# Optimizing a Trainium2 kernel written in Bass

```python
import numpy as np
import jax
import jax.numpy as jnp

def _softmax(x, axis=-1):
    return jax.nn.softmax(x, axis=axis)

def _gelu(x):
    return jax.nn.gelu(x, approximate=True)

def _silu(x):
    return jax.nn.silu(x)

def _sigmoid(x):
    return jax.nn.sigmoid(x)

def _layernorm(x, axis=-1, eps=1e-05):
    m = jnp.mean(x, axis=axis, keepdims=True)
    v = jnp.var(x, axis=axis, keepdims=True)
    return (x - m) / jnp.sqrt(v + eps)

def _scatter_add(tgt, idx, src, axis=0):
    return tgt.at[idx].add(src)

def _segment_sum(src, seg, n):
    return jax.ops.segment_sum(src, seg, n)
kernel_name = 'mk_metaformer_d1_conv_nhwc256_r4_3808c6'

def setup_inputs(seed: int=0):
    np.random.seed(seed)
    _w = jnp.asarray

    def _rec_inputs():
        import jax
        import jax.numpy as jnp
        _gk = jax.random.key(seed)
        x = -0.0003929 + 0.9999 * jax.random.normal(jax.random.fold_in(_gk, 1), (4, 32, 32, 64), jnp.float32)
        return x
    x = _rec_inputs()

    def _L0_conv_setup():
        import jax, jax.numpy as jnp
        import numpy as np
        from jax import lax

        def layer_norm(x, g, b, eps=1e-05):
            mu = jnp.mean(x, axis=-1, keepdims=True)
            var = jnp.var(x, axis=-1, keepdims=True)
            return (x - mu) / jnp.sqrt(var + eps) * g + b

        def selective_scan(u, delta, A, Bm, Cm, D):
            Bsz, L, d_inner = u.shape
            N = A.shape[1]

            def step(h, inp):
                u_t, d_t, B_t, C_t = inp
                dA = jnp.exp(d_t[..., None] * A)
                h = dA * h + (d_t * u_t)[..., None] * B_t[:, None, :]
                y = jnp.einsum('bdn,bn->bd', h, C_t)
                return (h, y)
            h0 = jnp.zeros((Bsz, d_inner, N), dtype=u.dtype)
            xs = (u.transpose(1, 0, 2), delta.transpose(1, 0, 2), Bm.transpose(1, 0, 2), Cm.transpose(1, 0, 2))
            _, ys = lax.scan(step, h0, xs)
            return ys.transpose(1, 0, 2) + u * D

        def mamba_block(x, in_proj_w, conv_w, conv_b, x_proj_w, dt_proj_w, dt_proj_b, A_log, D, out_proj_w):
            d_inner = in_proj_w.shape[0] // 2
            d_state = A_log.shape[1]
            dt_rank = dt_proj_w.shape[1]
            d_conv = conv_w.shape[-1]
            xz = x @ in_proj_w.T
            xi, z = jnp.split(xz, 2, axis=-1)
            xt = xi.transpose(0, 2, 1)
            kernel = conv_w[:, None, :]
            xc = lax.conv_general_dilated(xt, kernel, (1,), [(d_conv - 1, 0)], feature_group_count=d_inner, dimension_numbers=('NCH', 'OIH', 'NCH'))
            xc = xc + conv_b[None, :, None]
            xs = jax.nn.silu(xc).transpose(0, 2, 1)
            x_dbl = xs @ x_proj_w.T
            dt, Bm, Cm = jnp.split(x_dbl, [dt_rank, dt_rank + d_state], axis=-1)
            delta = jax.nn.softplus(dt @ dt_proj_w.T + dt_proj_b)
            A = -jnp.exp(A_log)
            y = selective_scan(xs, delta, A, Bm, Cm, D)
            y = y * jax.nn.silu(z)
            return y @ out_proj_w.T
        key = jax.random.key(seed)
        ks = jax.random.split(key, 12)
        B, H, W, C = (4, 32, 32, 64)
        d_state, d_conv, expand = (16, 4, 2)
        d_inner = expand * C
        dt_rank = int(np.ceil(C / 16))
        s = 0.02
        A = jnp.tile(jnp.arange(1, d_state + 1, dtype=jnp.float32)[None, :], (d_inner, 1))
        dt0 = jax.random.uniform(ks[9], (d_inner,), minval=0.001, maxval=0.1)
        return {'x': jax.random.normal(ks[0], (B, H, W, C), jnp.float32), 'ln_g': jnp.ones((C,), jnp.float32), 'ln_b': jnp.zeros((C,), jnp.float32), 'in_proj_w': jax.random.normal(ks[1], (2 * d_inner, C), jnp.float32) * s, 'conv_w': jax.random.normal(ks[2], (d_inner, d_conv), jnp.float32) * s, 'conv_b': jnp.zeros((d_inner,), jnp.float32), 'x_proj_w': jax.random.normal(ks[3], (dt_rank + 2 * d_state, d_inner), jnp.float32) * s, 'dt_proj_w': jax.random.normal(ks[4], (d_inner, dt_rank), jnp.float32) * dt_rank ** (-0.5), 'dt_proj_b': jnp.log(jnp.expm1(dt0)), 'A_log': jnp.log(A), 'D': jnp.ones((d_inner,), jnp.float32), 'out_proj_w': jax.random.normal(ks[5], (C, d_inner), jnp.float32) * s, 'proj_w': jax.random.normal(ks[6], (C, C), jnp.float32) * s, 'proj_b': jnp.zeros((C,), jnp.float32), 'skip_scale': jnp.ones((1,), jnp.float32)}
    _L0_conv_all = _L0_conv_setup()
    _L0_conv_in = {k: v for k, v in _L0_conv_all.items() if k in ('ln_g', 'ln_b', 'in_proj_w', 'conv_w', 'conv_b', 'x_proj_w', 'dt_proj_w', 'dt_proj_b', 'A_log', 'D', 'out_proj_w', 'proj_w', 'proj_b', 'skip_scale')}
    del _L0_conv_all

    def _L0_ffn_setup():
        import math
        import jax, jax.numpy as jnp
        import numpy as np
        CAPACITY_FACTOR = 1.25
        key = jax.random.key(seed)
        ks = jax.random.split(key, 5)
        B, L, D, F, E = (8, 2048, 64, 256, 8)
        h = jax.random.normal(ks[0], (B, L, D), dtype=jnp.float32)
        gate_w = jax.random.normal(ks[1], (D, E), dtype=jnp.float32) * 0.02
        gate_b = jnp.zeros((E,), dtype=jnp.float32)
        w1 = jax.random.normal(ks[2], (E, D, F), dtype=jnp.float32) * (1.0 / math.sqrt(D))
        b1 = jnp.zeros((E, F), dtype=jnp.float32)
        w2 = jax.random.normal(ks[3], (E, F, D), dtype=jnp.float32) * (1.0 / math.sqrt(F))
        b2 = jnp.zeros((E, D), dtype=jnp.float32)
        return {'h': h, 'gate_w': gate_w, 'gate_b': gate_b, 'w1': w1, 'b1': b1, 'w2': w2, 'b2': b2}
    _L0_ffn_all = _L0_ffn_setup()
    _L0_ffn_in = {k: v for k, v in _L0_ffn_all.items() if k in ('gate_w', 'gate_b', 'w1', 'b1', 'w2', 'b2')}
    del _L0_ffn_all
    return {'x': x, 'L0_conv_ln_g': _L0_conv_in['ln_g'], 'L0_conv_ln_b': _L0_conv_in['ln_b'], 'L0_conv_in_proj_w': _L0_conv_in['in_proj_w'], 'L0_conv_conv_w': _L0_conv_in['conv_w'], 'L0_conv_conv_b': _L0_conv_in['conv_b'], 'L0_conv_x_proj_w': _L0_conv_in['x_proj_w'], 'L0_conv_dt_proj_w': _L0_conv_in['dt_proj_w'], 'L0_conv_dt_proj_b': _L0_conv_in['dt_proj_b'], 'L0_conv_A_log': _L0_conv_in['A_log'], 'L0_conv_D': _L0_conv_in['D'], 'L0_conv_out_proj_w': _L0_conv_in['out_proj_w'], 'L0_conv_proj_w': _L0_conv_in['proj_w'], 'L0_conv_proj_b': _L0_conv_in['proj_b'], 'L0_conv_skip_scale': _L0_conv_in['skip_scale'], 'L0_ffn_gate_w': _L0_ffn_in['gate_w'], 'L0_ffn_gate_b': _L0_ffn_in['gate_b'], 'L0_ffn_w1': _L0_ffn_in['w1'], 'L0_ffn_b1': _L0_ffn_in['b1'], 'L0_ffn_w2': _L0_ffn_in['w2'], 'L0_ffn_b2': _L0_ffn_in['b2']}

def reference(x, L0_conv_ln_g, L0_conv_ln_b, L0_conv_in_proj_w, L0_conv_conv_w, L0_conv_conv_b, L0_conv_x_proj_w, L0_conv_dt_proj_w, L0_conv_dt_proj_b, L0_conv_A_log, L0_conv_D, L0_conv_out_proj_w, L0_conv_proj_w, L0_conv_proj_b, L0_conv_skip_scale, L0_ffn_gate_w, L0_ffn_gate_b, L0_ffn_w1, L0_ffn_b1, L0_ffn_w2, L0_ffn_b2):
    import jax
    import jax.numpy as jnp

    def _L0_conv_ref(x, ln_g, ln_b, in_proj_w, conv_w, conv_b, x_proj_w, dt_proj_w, dt_proj_b, A_log, D, out_proj_w, proj_w, proj_b, skip_scale):
        import jax, jax.numpy as jnp
        import numpy as np
        from jax import lax

        def layer_norm(x, g, b, eps=1e-05):
            mu = jnp.mean(x, axis=-1, keepdims=True)
            var = jnp.var(x, axis=-1, keepdims=True)
            return (x - mu) / jnp.sqrt(var + eps) * g + b

        def selective_scan(u, delta, A, Bm, Cm, D):
            Bsz, L, d_inner = u.shape
            N = A.shape[1]

            def step(h, inp):
                u_t, d_t, B_t, C_t = inp
                dA = jnp.exp(d_t[..., None] * A)
                h = dA * h + (d_t * u_t)[..., None] * B_t[:, None, :]
                y = jnp.einsum('bdn,bn->bd', h, C_t)
                return (h, y)
            h0 = jnp.zeros((Bsz, d_inner, N), dtype=u.dtype)
            xs = (u.transpose(1, 0, 2), delta.transpose(1, 0, 2), Bm.transpose(1, 0, 2), Cm.transpose(1, 0, 2))
            _, ys = lax.scan(step, h0, xs)
            return ys.transpose(1, 0, 2) + u * D

        def mamba_block(x, in_proj_w, conv_w, conv_b, x_proj_w, dt_proj_w, dt_proj_b, A_log, D, out_proj_w):
            d_inner = in_proj_w.shape[0] // 2
            d_state = A_log.shape[1]
            dt_rank = dt_proj_w.shape[1]
            d_conv = conv_w.shape[-1]
            xz = x @ in_proj_w.T
            xi, z = jnp.split(xz, 2, axis=-1)
            xt = xi.transpose(0, 2, 1)
            kernel = conv_w[:, None, :]
            xc = lax.conv_general_dilated(xt, kernel, (1,), [(d_conv - 1, 0)], feature_group_count=d_inner, dimension_numbers=('NCH', 'OIH', 'NCH'))
            xc = xc + conv_b[None, :, None]
            xs = jax.nn.silu(xc).transpose(0, 2, 1)
            x_dbl = xs @ x_proj_w.T
            dt, Bm, Cm = jnp.split(x_dbl, [dt_rank, dt_rank + d_state], axis=-1)
            delta = jax.nn.softplus(dt @ dt_proj_w.T + dt_proj_b)
            A = -jnp.exp(A_log)
            y = selective_scan(xs, delta, A, Bm, Cm, D)
            y = y * jax.nn.silu(z)
            return y @ out_proj_w.T
        B, H, W, C = x.shape
        xc = x.transpose(0, 3, 1, 2)
        L = H * W
        x_flat = xc.reshape(B, C, L).transpose(0, 2, 1)
        x_norm = layer_norm(x_flat, ln_g, ln_b)
        y = mamba_block(x_norm, in_proj_w, conv_w, conv_b, x_proj_w, dt_proj_w, dt_proj_b, A_log, D, out_proj_w)
        y = y + skip_scale * x_norm
        y = layer_norm(y, ln_g, ln_b)
        y = y @ proj_w.T + proj_b
        out = y.transpose(0, 2, 1).reshape(B, -1, H, W)
        return out.transpose(0, 2, 3, 1)

    def _L0_ffn_ref(h, gate_w, gate_b, w1, b1, w2, b2):
        import math
        import jax, jax.numpy as jnp
        import numpy as np
        CAPACITY_FACTOR = 1.25
        B, L, D = h.shape
        E = gate_w.shape[1]
        T = B * L
        C = max(1, math.ceil(CAPACITY_FACTOR * T / E))
        x = h.reshape(T, D)
        logits = x @ gate_w + gate_b
        probs = jax.nn.softmax(logits, axis=-1)
        idx = jnp.argmax(probs, axis=-1)
        prb = jnp.take_along_axis(probs, idx[:, None], axis=1)[:, 0]
        one_hot = jax.nn.one_hot(idx, E, dtype=jnp.float32)
        pos = (jnp.cumsum(one_hot, axis=0) * one_hot).sum(-1).astype(jnp.int32) - 1
        kept = pos < C
        pos_safe = jnp.where(kept, pos, C)
        buf = jnp.zeros((E, C, D), dtype=h.dtype).at[idx, pos_safe].set(x, mode='drop')
        hmid = jax.nn.relu(jnp.einsum('ecd,edf->ecf', buf, w1) + b1[:, None, :])
        ybuf = jnp.einsum('ecf,efd->ecd', hmid, w2) + b2[:, None, :]
        pos_g = jnp.minimum(pos, C - 1)
        y_tok = ybuf[idx, pos_g] * (prb * kept)[:, None]
        y = y_tok.reshape(B, L, D)
        y = jnp.nan_to_num(y, nan=0.0, posinf=10000.0, neginf=-10000.0)
        return y

    def _gn(v, G=32, eps=1e-05):
        B_, H_, W_, C_ = v.shape
        g = v.reshape(B_, H_, W_, G, C_ // G)
        m = jnp.mean(g, axis=(1, 2, 4), keepdims=True)
        s = jnp.var(g, axis=(1, 2, 4), keepdims=True)
        return ((g - m) / jnp.sqrt(s + eps)).reshape(v.shape)

    def _ln_c(v, eps=1e-06):
        m = jnp.mean(v, axis=-1, keepdims=True)
        s = jnp.var(v, axis=-1, keepdims=True)
        return (v - m) / jnp.sqrt(s + eps)

    def _ln_t(v, eps=1e-05):
        m = jnp.mean(v, axis=-1, keepdims=True)
        s = jnp.var(v, axis=-1, keepdims=True)
        return (v - m) / jnp.sqrt(s + eps)

    def _to_tokens(v):
        B_, H_, W_, C_ = v.shape
        return v.reshape(B_, H_ * W_, C_)

    def _from_tokens(t, like):
        return t.reshape(like.shape)
    x = x + _L0_conv_ref(_ln_c(x), L0_conv_ln_g, L0_conv_ln_b, L0_conv_in_proj_w, L0_conv_conv_w, L0_conv_conv_b, L0_conv_x_proj_w, L0_conv_dt_proj_w, L0_conv_dt_proj_b, L0_conv_A_log, L0_conv_D, L0_conv_out_proj_w, L0_conv_proj_w, L0_conv_proj_b, L0_conv_skip_scale)
    t = _to_tokens(x)
    t = t + _L0_ffn_ref(_ln_t(t), L0_ffn_gate_w, L0_ffn_gate_b, L0_ffn_w1, L0_ffn_b1, L0_ffn_w2, L0_ffn_b2)
    x = _from_tokens(t, x)
    return x

_drawn_inputs = setup_inputs


def setup_inputs(seed=0):
    import zlib

    import numpy as np

    out = dict(_drawn_inputs(seed))
    spreads = {'L0_conv_ln_g': (1.0, 0.2),
     'L0_conv_ln_b': (0.0, 0.1),
     'L0_conv_conv_b': (0.0, 0.8),
     'L0_conv_D': (1.0, 0.6),
     'L0_conv_proj_b': (0.0, 0.1),
     'L0_ffn_gate_b': (0.0, 0.1),
     'L0_ffn_b1': (0.0, 0.8),
     'L0_ffn_b2': (0.0, 0.694)}
    factors = {'L0_conv_in_proj_w': 8.0,
     'L0_conv_conv_w': 8.0,
     'L0_conv_x_proj_w': 8.0,
     'L0_conv_dt_proj_w': 8.0,
     'L0_conv_dt_proj_b': 8.0,
     'L0_conv_A_log': 8.0,
     'L0_conv_out_proj_w': 8.0}
    for name, (base, spread) in spreads.items():
        noise = np.random.default_rng([zlib.crc32(name.encode()), seed]).standard_normal(out[name].shape)
        drawn = base * np.exp(spread * noise) if base else spread * noise
        out[name] = jnp.asarray(drawn.astype(out[name].dtype))
    for name, factor in factors.items():
        out[name] = (out[name] * factor).astype(out[name].dtype)
    return out
```

```python
from contextlib import ExitStack

import concourse.bass as bass
from concourse import mybir

ALU = mybir.AluOpType
ACT = mybir.ActivationFunctionType
AX = mybir.AxisListType.X
F32 = mybir.dt.float32
BF16 = mybir.dt.bfloat16
I32 = mybir.dt.int32

P = 128
B, H, W, C = 4, 32, 32, 64
L = H * W
T = L // P
DI = 2 * C
N = 16
R = 4
TAPS = 4
HALF = 512
E, F = 8, 256
CAP = (B * L * 5 // 4 + E - 1) // E
ET = CAP // P
LN_C_EPS, LN_EPS = 1e-6, 1e-5

R_ONE, R_RES, R_PRB, R_ID, ROW = C, C + 1, 2 * C + 1, 2 * C + 2, 2 * C + 3
NOWHERE = 1 << 20
SENT = 16 * (T + 1)


class Chain:

    def __init__(self, eng, sem, turn, steps):
        self.eng, self.sem, self.base, self.steps, self.n = eng, sem, turn * steps, steps, 0

    def __call__(self, ins):
        self.n += 1
        assert self.n <= self.steps
        ins.then_inc(self.sem, 1)
        self.eng.wait_ge(self.sem, self.base + self.n)

    def end(self):
        assert self.n == self.steps, (self.n, self.steps)


def metaformer_layer(nc, x, ln_g, ln_b, in_proj_w, conv_w, conv_b, x_proj_w, dt_proj_w, dt_proj_b, A_log,
                     D, out_proj_w, proj_w, proj_b, skip_scale, gate_w, gate_b, w1, b1, w2, b2, out):
    x_dram = x.rearrange("b h w c -> (b h w) c").rearrange("(b t p) c -> b p t c", b=B, p=P)
    out_rows = out.rearrange("b h w c -> (b h w) c")
    out_dram = out_rows.rearrange("(b t p) c -> b p t c", b=B, p=P)
    slots_dram = nc.dram_tensor("slots", (E * CAP, ROW), F32, kind="Internal").ap()

    with ExitStack() as ctx:
        def sb(name, shape, dt=F32):
            return ctx.enter_context(nc.sbuf_tensor(name, shape, dt))

        def sem(name):
            return ctx.enter_context(nc.semaphore(name))

        Bp = ctx.enter_context(nc.psum_tensor("Bp", [P, L], F32))
        Cp = ctx.enter_context(nc.psum_tensor("Cp", [P, L], F32))
        Yp = ctx.enter_context(nc.psum_tensor("Yp", [P, L], F32))
        M0 = ctx.enter_context(nc.psum_tensor("M0", [P, HALF], F32))
        M1 = ctx.enter_context(nc.psum_tensor("M1", [P, HALF], F32))

        ident = sb("ident", [P, P])
        sel1 = sb("sel1", [96, 2 * N], BF16)
        sel = sb("sel", [96, 2 * N, P], BF16)
        tri = sb("tri", [P, P], BF16)
        ones = sb("ones", [P, P], BF16)
        revc = sb("revc", [P, T, E])
        revi = sb("revi", [P, T, E], I32)
        ids = sb("ids", [P, B, T], I32)
        resets = sb("resets", [P, E, T + 1])
        mhalf = sb("mhalf", [P, T])
        invC = sb("invC", [P, T])
        zero = sb("zero", [P, T], I32)
        eps6 = sb("eps6", [P, T])
        eps5 = sb("eps5", [P, T])
        gcol = sb("gcol", [C, 1])
        bcol = sb("bcol", [C, 1])
        cw = sb("cw", [P, TAPS])
        cb = sb("cb", [P, 1])
        xbc3 = sb("xbc3", [96, P])
        xdt = sb("xdt", [R, P])
        dtw = sb("dtw", [P, R])
        dtb = sb("dtb", [P, 1])
        alog = sb("alog", [P, N])
        aneg = sb("aneg", [P, N])
        Dcol = sb("Dcol", [P, 1])
        wo = sb("wo", [C, P])
        pw = sb("pw", [C, C])
        pb = sb("pb", [1, C])
        last1 = sb("last1", [1, C + 1])
        gfold = sb("gfold", [C, C + 1])
        skcol = sb("skcol", [C, 1])
        skipI = sb("skipI", [C, C])
        gw = sb("gw", [C + 1, E])
        w1s = sb("w1s", [C, E, F])
        w2s = sb("w2s", [P, E, 2, C])
        b1r = sb("b1r", [2 * E, P])
        b1c = sb("b1c", [P, 2 * E])
        b2s = sb("b2s", [P, E, C])
        tapA = sb("tapA", [P, P])
        tapB = sb("tapB", [P, P])
        wzT = sb("wzT", [C, P])
        bcT = sb("bcT", [P, 96])
        dtwT = sb("dtwT", [R, P])
        woT = sb("woT", [P, C])
        pwT = sb("pwT", [C, C])
        wdt = sb("wdt", [P, P])
        PW = sb("PW", [C + 1, C])

        xs_in = sb("xs_in", [P, B, T, C])
        u = sb("u", [P, B, L])
        sz = sb("sz", [P, B, L])
        delta = sb("delta", [P, L])
        du = sb("du", [P, B, L])
        parts = sb("parts", [96, B, L], BF16)
        skx = sb("skx", [P, B, T, C])

        fs = sb("fs", [P, 10, T])
        fxm = sb("fxm", [P, T, C])
        fz = sb("fz", [P, T, C + 1])
        xnT = sb("xnT", [P, L + 3])
        r1 = sb("r1", [96, L])
        mid = sb("mid", [96, L], BF16)
        tabs = sb("tabs", [P, L])
        trel = sb("trel", [P, L])
        te = sb("te", [P, L])
        dA = sb("dA", [P, 3, L])
        h = sb("h", [P, 4, L])
        prod = sb("prod", [P, 4, L])
        csb = sb("csb", [P, 2, L])
        yt = sb("yt", [P, L])
        bs = sb("bs", [P, 28, T])
        y2 = sb("y2", [P, T, C])
        bxm = sb("bxm", [P, T, C])
        n2 = sb("n2", [P, T, C + 1])
        bT = sb("bT", [C + 1, L])
        rows = sb("rows", [P, T, ROW])
        ld = sb("ld", [P, T, E])
        lex = sb("lex", [P, T, E])
        lrev = sb("lrev", [P, T, E])
        lpo = sb("lpo", [P, T, E])
        oh = sb("oh", [P, E, T + 1], BF16)
        before = sb("before", [P, E, T + 1], BF16)
        chosen = sb("chosen", [P, T], I32)
        slot = sb("slot", [P, T], I32)
        fill = sb("fill", [P, ROW])
        def within(buf, start, *dims):
            size = 1
            for d in dims:
                size *= d
            flat = buf[:, :, :].rearrange("p a l -> p (a l)")[:, start:start + size]
            names = "abcd"[:len(dims)]
            if len(dims) == 1:
                return flat
            return flat.rearrange(f"p ({' '.join(names)}) -> p {' '.join(names)}",
                                  **{k: d for k, d in zip(names[1:], dims[1:])})

        wi = within(dA, 0, 2, C)
        taps = within(dA, L, TAPS, C)
        xe = within(h, 0, 3, ET, ROW)
        xT = within(prod, 0, CAP)[0:C]
        h0 = within(prod, L, CAP)
        h1 = within(prod, 2 * L, CAP)
        ye = within(dA, 0, 4, ET, C)
        yo = within(prod, 3 * L, 2, ET, C)
        fin = within(dA, 2 * L, ET, C).bitcast(I32)

        x_first, x_rest = sem("x_first"), sem("x_rest")
        w_in, late_in = sem("w_in"), sem("late_in")
        pool_const, pool_init = sem("pool_const"), sem("pool_init")
        sel_done, taps_done = sem("sel_done"), sem("taps_done")
        w_tr, w_ev, w_mm, w_ready, aneg_done, a_exp = (sem("w_tr"), sem("w_ev"), sem("w_mm"), sem("w_ready"),
                                                       sem("aneg_done"), sem("a_exp"))
        (f_sum, f_xm, f_sq, f_var, f_z, f_tr, f_top, f_bot, f_mx, f_xcr, f_mz, f_zr, f_silu, f_sk, f_skx,
         f_bc, f_hi, f_r1, f_rest, f_mid, f_parts, f_dt, f_am, f_exp, f_ln, f_lm, f_corr, f_delta, f_du, f_mean, f_rstd) = map(sem, (
             "f_sum f_xm f_sq f_var f_z f_tr f_top f_bot f_mx f_xcr f_mz f_zr f_silu f_sk f_skx "
             "f_bc f_hi f_r1 f_rest f_mid f_parts f_dt f_am f_exp f_ln f_lm f_corr f_delta f_du f_mean f_rstd").split())
        s_B, s_mul, s_dA, s_scan, s_C, s_ccp, s_pD, s_pP, s_sum = map(sem, (
            "s_B s_mul s_dA s_scan s_C s_ccp s_pD s_pP s_sum").split())
        (b_yt, b_yg, b_op, b_y2, b_sum, b_xm, b_sq, b_var, b_n2, b_tr, b_n2T, b_pr, b_t1, b_sum3, b_xm3, b_sq3,
         b_var3, b_h3, b_tr3, b_h3T, b_gate, b_ld, b_ex, b_oh, b_pos, b_idx, b_pool, b_dve, b_dve2, b_dve3, b_sent) = map(sem, (
             "b_yt b_yg b_op b_y2 b_sum b_xm b_sq b_var b_n2 b_tr b_n2T b_pr b_t1 b_sum3 b_xm3 b_sq3 "
             "b_var3 b_h3 b_tr3 b_h3T b_gate b_ld b_ex b_oh b_pos b_idx b_pool b_dve b_dve2 b_dve3 b_sent").split())
        fill_done = sem("fill_done")
        e_in = [sem(f"e_in{i}") for i in range(3)]
        e_out = [sem(f"e_out{i}") for i in range(3)]
        e_tr, e_xT, e_up, e_h0, e_h1, e_dn, e_yo, e_dve, e_diff = map(sem, (
            "e_tr e_xT e_up e_h0 e_h1 e_dn e_yo e_dve e_diff").split())

        def at(buf, b):
            return buf[:, bass.ds(b, 1), :].rearrange("p b l -> p (b l)")

        def at_half(buf, b, q):
            return buf[:, bass.ds(b, 1), q * HALF:(q + 1) * HALF].rearrange("p b l -> p (b l)")

        def at_tiles(buf, b):
            return buf[:, bass.ds(b, 1), :, :].rearrange("p b t c -> p (b t) c")

        def over(col, n):
            return col.unsqueeze(2).broadcast_to([P, col.shape[1], n])

        def first(b):
            return isinstance(b, int) and b == 0

        def tiles(psum, n, k=T):
            return psum.rearrange("p (t c) -> p t c", t=k)[:, :, 0:n]

        block = ctx.enter_context(nc.Block())
        HB = [slice(0, HALF), slice(HALF, L)]

        @block.sync
        def _(sp):
            sp.dma_start(xs_in[:, 0], x_dram[0]).then_inc(x_first, 16)
            for dst, src in ((wi[:, :, :], in_proj_w.rearrange("(h p) c -> p h c", p=P)),
                             (cw[:, :], conv_w),
                             (gcol[:, :], ln_g.unsqueeze(1)), (bcol[:, :], ln_b.unsqueeze(1)),
                             (cb[:, :], conv_b.unsqueeze(1)), (dtb[:, :], dt_proj_b.unsqueeze(1)),
                             (xbc3[0:32, :], x_proj_w[R:R + 2 * N, :]), (xbc3[32:64, :], x_proj_w[R:R + 2 * N, :]),
                             (xbc3[64:96, :], x_proj_w[R:R + 2 * N, :]), (xdt[:, :], x_proj_w[0:R, :]),
                             (dtw[:, :], dt_proj_w), (alog[:, :], A_log), (Dcol[:, :], D.unsqueeze(1)),
                             (wo[:, :], out_proj_w), (pw[:, :], proj_w), (pb[:, :], proj_b.unsqueeze(0)),
                             (skcol[:, :], skip_scale.unsqueeze(0).broadcast_to([C, 1])),
                             (b1r[:, :], b1.rearrange("e (h f) -> (e h) f", h=2))):
                sp.dma_start(dst, src).then_inc(w_in, 16)
            sp.dma_start(xs_in[:, 1:B], x_dram[1:B].rearrange("b p t c -> p b t c")).then_inc(x_rest, 16)
            for dst, src in ((gw[0:C, :], gate_w), (gw[C:C + 1, :], gate_b.unsqueeze(0)),
                             (w1s[:, :, :], w1.rearrange("e c f -> c e f")),
                             (w2s[:, :, :, :], w2.rearrange("e (h f) c -> f e h c", h=2)),
                             (b2s[:, :, :], b2.unsqueeze(0).broadcast_to([P, E, C]))):
                sp.dma_start(dst, src).then_inc(late_in, 16)
            sp.wait_ge(b_sent, 16 + SENT * B)
            for e in range(E):
                if e >= 3:
                    sp.wait_ge(e_out[e % 3], 16 * ET * (e // 3))
                sp.dma_start(xe[:, e % 3],
                             slots_dram[e * CAP:(e + 1) * CAP, :].rearrange("(k p) r -> p k r", p=P)
                             ).then_inc(e_in[e % 3], 16)

        @block.gpsimd
        def _(pool):
            po = nc.gpsimd
            po.memset(ident[:, :], 0.0).then_inc(pool_init, 1)
            po.memset(sel1[:, :], 0.0).then_inc(pool_init, 1)
            po.memset(tri[:, :], 1.0).then_inc(pool_init, 1)
            po.memset(ones[:, :], 1.0)
            po.memset(mhalf[:, :], -0.5)
            po.memset(invC[:, :], 1.0 / C)
            po.memset(zero[:, :], 0)
            po.memset(eps6[:, :], LN_C_EPS)
            po.memset(eps5[:, :], LN_EPS)
            po.memset(resets[:, :, :], 1.0)
            po.memset(last1[:, :], 0.0)
            po.memset(n2[:, :, C:C + 1], 1.0)
            po.memset(fz[:, :, C:C + 1], 1.0)
            po.memset(rows[:, :, R_ONE:R_ONE + 1], 1.0)
            po.memset(xnT[:, 0:3], 0.0)
            po.memset(oh[:, :, 0:1], 0.0)
            po.memset(fill[:, :], 0.0).then_inc(fill_done, 1)
            po.iota(revi[:, :, :], pattern=[[0, T], [-1, E]], base=E, channel_multiplier=0)
            po.iota(ids[:, :, :], pattern=[[L, B], [P, T]], base=0, channel_multiplier=1).then_inc(pool_init, 1)
            pool.wait_ge(pool_init, 4)
            pool.wait_ge(fill_done, 1)
            po.affine_select(out=ident[:, :], in_=ident[:, :], compare_op=ALU.not_equal, fill=1.0, base=0,
                             pattern=[[-1, P]], channel_multiplier=1)
            po.iota(fill[:, R_ID:R_ID + 1].bitcast(I32), pattern=[[0, 1]], base=NOWHERE,
                    channel_multiplier=0).then_inc(fill_done, 1)
            po.affine_select(out=tri[:, :], in_=tri[:, :], compare_op=ALU.is_gt, fill=0.0, base=0,
                             pattern=[[1, P]], channel_multiplier=-1)
            po.memset(resets[:, :, 0:1], 0.0)
            po.memset(last1[:, C:C + 1], 1.0)
            for k in range(3):
                po.affine_select(out=sel1[:, :], in_=sel1[:, :], compare_op=ALU.not_equal, fill=1.0, base=-32 * k,
                                 pattern=[[-1, 2 * N]], channel_multiplier=1).then_inc(pool_const, 1)
                pool.wait_ge(pool_const, k + 1)
            po.tensor_copy(revc[:, :, :], revi[:, :, :]).then_inc(pool_const, 1)
            pool.wait_ge(pool_const, 4)
            pool.wait_ge(fill_done, 2)
            po.dma_start(slots_dram.rearrange("(k p) r -> p k r", p=P),
                         fill[:, :].unsqueeze(1).broadcast_to([P, E * ET, ROW])).then_inc(b_sent, 16)

            def rstd(link, s, var_sum, o, eps):
                link(po.tensor_tensor(s[:, o, :], s[:, var_sum, :], invC[:, :], ALU.mult))
                link(po.tensor_tensor(s[:, o + 1, :], s[:, o, :], eps[:, :], ALU.add))
                link(po.tensor_tensor(s[:, o + 2, :], s[:, o + 1, :], mhalf[:, :], ALU.pow))

            def front(f, n):
                if n == 0:
                    if not first(f):
                        pool.wait_ge(f_du, f)
                        pool.wait_ge(f_parts, 2 * f)
                    link = Chain(pool, f_mean, f, 1)
                    pool.wait_ge(f_sum, f + 1)
                    link(po.tensor_tensor(fs[:, 1, :], fs[:, 0, :], invC[:, :], ALU.mult))
                    po.tensor_tensor(fxm[:, :, :], at_tiles(xs_in, f), over(fs[:, 1, :], C),
                                     ALU.subtract).then_inc(f_xm, 1)
                if n == 2:
                    pool.wait_ge(f_var, f + 1)
                    link = Chain(pool, f_rstd, f, 8)
                    rstd(link, fs, 2, 3, eps6)
                    link(po.tensor_tensor(fs[:, 6, :], fs[:, 3, :], fs[:, 5, :], ALU.mult))
                    link(po.tensor_tensor(fs[:, 7, :], fs[:, 6, :], fs[:, 5, :], ALU.mult))
                    link(po.tensor_tensor(fs[:, 8, :], fs[:, 7, :], eps5[:, :], ALU.add))
                    link(po.tensor_tensor(fs[:, 9, :], fs[:, 8, :], mhalf[:, :], ALU.pow))
                    link(po.tensor_tensor(fs[:, 0, :], fs[:, 9, :], fs[:, 5, :], ALU.mult))
                    link.end()
                    po.tensor_tensor(fz[:, :, 0:C], fxm[:, :, :], over(fs[:, 0, :], C), ALU.mult).then_inc(f_z, 1)
                if n == 14:
                    pool.wait_ge(f_ln, f + 1)
                    po.tensor_tensor(tabs[:, :], tabs[:, :], trel[:, :], ALU.add).then_inc(f_lm, 1)

            def scan(s, n):
                j = n // 2
                pool.wait_ge(s_ccp, 8 * s + j + 1)
                pool.wait_ge(s_scan, 16 * s + n + 1)
                if not (first(s) and j < 2):
                    pool.wait_ge(s_sum, 16 * s + n - 3)
                po.tensor_tensor(prod[:, 2 + j % 2, :], h[:, 2 + j % 2, :], csb[:, j % 2, :],
                                 ALU.mult).then_inc(s_pP, 1)

            def back(g, n):
                if n == 0:
                    pool.wait_ge(b_yt, g + 1)
                    pool.wait_ge(f_silu, g + 1)
                    po.tensor_tensor(yt[:, :], yt[:, :], at(sz, g), ALU.mult).then_inc(b_yg, 1)
                if n in (3, 9):
                    k = 0 if n == 3 else 1
                    pool.wait_ge((b_sum, b_sum3)[k], g + 1)
                    o = 10 * k
                    link = Chain(pool, b_pool, 2 * g + k, 4)
                    link(po.tensor_tensor(bs[:, o + 1, :], bs[:, o, :], invC[:, :], ALU.mult))
                    src = (y2[:, :, :], rows[:, :, R_RES:R_RES + C])[k]
                    po.tensor_tensor(bxm[:, :, :], src, over(bs[:, o + 1, :], C),
                                     ALU.subtract).then_inc((b_xm, b_xm3)[k], 1)
                    links[k] = link
                if n in (5, 11):
                    k = 0 if n == 5 else 1
                    o = 10 * k
                    pool.wait_ge((b_var, b_var3)[k], g + 1)
                    link = links[k]
                    rstd(link, bs, o + 2, o + 3, eps5)
                    link.end()
                    dst = (n2[:, :, 0:C], rows[:, :, 0:C])[k]
                    po.tensor_tensor(dst, bxm[:, :, :], over(bs[:, o + 5, :], C),
                                     ALU.mult).then_inc((b_n2, b_h3)[k], 1)
                if n == 16:
                    pool.wait_ge(b_idx, g + 1)
                    po.tensor_tensor(slot[:, :], chosen[:, :], zero[:, :], ALU.add)
                    pool.drain()
                    po.dma_start(out_dram[bass.ds(g, 1)].rearrange("b p t c -> p (b t) c"),
                                 rows[:, :, R_RES:R_RES + C]).then_inc(b_sent, 16)
                    for t in range(T):
                        po.indirect_dma_start(slots_dram[:, :], bass.IndirectOffsetOnAxis(ap=slot[:, t:t + 1], axis=0),
                                              rows[:, t, :], None, bounds_check=last_slot,
                                              oob_is_err=False).then_inc(b_sent, 16)

            links = [None, None]
            last_slot = po.to_reg(E * CAP - 1)
            for n in range(17):
                front(0, n)

            def step(s, has_front, has_back):
                for n in range(16):
                    if has_back:
                        back(s - 1, n)
                    if n % 2:
                        scan(s, n)
                    if has_front:
                        front(s + 1, n)
                if has_back:
                    back(s - 1, 16)

            step(0, True, False)
            with pool.Fori(1, B - 1) as s:
                step(s, True, True)
            step(B - 1, False, True)
            for n in range(17):
                back(B - 1, n)
            pool.wait_ge(b_sent, 16 + SENT * B)
            for e in range(E):
                pool.wait_ge(e_yo, e + 1)
                for k in range(ET):
                    po.indirect_dma_start(out_rows, bass.IndirectOffsetOnAxis(
                        ap=xe[:, e % 3, k, R_ID:R_ID + 1].bitcast(I32), axis=0), yo[:, e % 2, k, :], None,
                        bounds_check=B * L - 1, oob_is_err=False).then_inc(e_out[e % 3], 16)
            for i in range(3):
                pool.wait_ge(e_out[i], 16 * ET * len(range(i, E, 3)))

        @block.scalar
        def _(act):
            ac = nc.scalar

            def act_set():
                ac.preload_act_table_set("natural_log_exp_and_others")

            def front(f, n):
                if n == 0 and not first(f):
                    act.wait_ge(f_du, f)
                    act.wait_ge(f_parts, 2 * f)
                if n == 1:
                    act.wait_ge(f_xm, f + 1)
                    ac.activation(fz[:, :, 0:C], fxm[:, :, :], ACT.Square).then_inc(f_sq, 1)
                if n in (3, 4):
                    q = n - 3
                    act.wait_ge(f_tr, 2 * f + q + 1)
                    ac.activation(xnT[0:C, 3 + q * HALF:3 + (q + 1) * HALF], M0[0:C, :], ACT.Identity,
                                  bias=bcol[:, :], scale=gcol[:, :]).then_inc(f_top, 1)
                if n in (5, 6):
                    q = n - 5
                    act.wait_ge(f_mx, 2 * f + q + 1)
                    ac.activation(at_half(u, f, q), M0[:, :], ACT.Identity, bias=cb[:, :]).then_inc(f_xcr, 1)
                if n in (7, 8):
                    q = n - 7
                    act.wait_ge(f_mz, 2 * f + q + 1)
                    ac.activation(at_half(sz, f, q), M0[:, :], ACT.Copy).then_inc(f_zr, 1)
                if n == 9:
                    act.wait_ge(f_sk, f + 1)
                    ac.activation(at_tiles(skx, f), tiles(M0[:, :], C), ACT.Copy).then_inc(f_skx, 1)
                    act.drain()
                    ac.activation(at(u, f), at(u, f), ACT.Silu)
                    ac.activation(at(sz, f), at(sz, f), ACT.Silu).then_inc(f_silu, 1)
                    act_set()
                if n in (10, 11):
                    q = n - 10
                    act.wait_ge(f_bc, 2 * f + q + 1)
                    ac.activation(at_half(parts, f, q), M0[0:96, :], ACT.Copy).then_inc(f_hi, 1)
                if n in (12, 13):
                    q = n - 12
                    act.wait_ge(f_r1, 2 * f + q + 1)
                    ac.activation(at_half(parts, f, q)[32:64], r1[32:64, HB[q]], ACT.Copy).then_inc(f_mid, 1)
                    act.wait_ge(f_dt, 2 * f + q + 1)
                    ac.activation(tabs[:, HB[q]], M0[:, :], ACT.Abs, bias=dtb[:, :])
                    ac.activation(trel[:, HB[q]], M0[:, :], ACT.Relu, bias=dtb[:, :]).then_inc(f_am, 1)
                    if q == 1:
                        act.wait_ge(f_am, 2 * f + 2)
                        ac.activation(te[:, :], tabs[:, :], ACT.Exp, scale=-1.0).then_inc(f_exp, 1)
                        act.wait_ge(f_exp, f + 1)
                        ac.activation(tabs[:, :], te[:, :], ACT.Ln, bias=1.0).then_inc(f_ln, 1)

            def decay(s, n):
                if not (first(s) and n < 3):
                    act.wait_ge(s_scan, 16 * s + n - 2)
                ac.activation(dA[:, n % 3, :], delta[:, :], ACT.Exp, scale=aneg[:, n:n + 1]).then_inc(s_dA, 1)

            def scan(s, n):
                if n + 2 < 16:
                    decay(s, n + 2)
                if n % 2:
                    j = n // 2
                    act.wait_ge(s_C, 16 * s + n + 1)
                    if not (first(s) and j < 2):
                        act.wait_ge(s_pP, 8 * s + j - 1)
                    ac.activation(csb[:, j % 2, :], Cp[:, :], ACT.Copy).then_inc(s_ccp, 1)

            def back(g, n):
                if n in (4, 10):
                    k = 0 if n == 4 else 1
                    act.wait_ge((b_xm, b_xm3)[k], g + 1)
                    ac.activation((n2, rows)[k][:, :, 0:C], bxm[:, :, :], ACT.Square).then_inc((b_sq, b_sq3)[k], 1)
                if n in (6, 7, 12, 13):
                    k, q = n // 8, (n - 6) % 2
                    act.wait_ge((b_tr, b_tr3)[k], 2 * g + q + 1)
                    ac.activation(bT[:, HB[q]], M1[0:C + 1, :], ACT.Copy).then_inc((b_n2T, b_h3T)[k], 1)
                if n == 15:
                    act.wait_ge(b_ld, g + 1)
                    ac.activation(lex[:, :, :], ld[:, :, :], ACT.Exp).then_inc(b_ex, 1)

            act_set()
            act.wait_ge(w_in, 16 * 18)
            ac.activation(aneg[:, :], alog[:, :], ACT.Exp).then_inc(a_exp, 1)
            for n in range(17):
                front(0, n)
            act.wait_ge(aneg_done, 1)

            def step(s, has_front, has_back):
                act.wait_ge(f_delta, s + 1)
                decay(s, 0)
                decay(s, 1)
                for n in range(16):
                    scan(s, n)
                    if has_back:
                        back(s - 1, n)
                    if has_front:
                        front(s + 1, n)

            step(0, True, False)
            with act.Fori(1, B - 1) as s:
                step(s, True, True)
            step(B - 1, False, True)
            for n in range(17):
                back(B - 1, n)
            for e in range(E):
                act.wait_ge(e_tr, e + 1)
                if e:
                    act.wait_ge(e_up, 2 * e)
                ac.activation(xT[:, :], Bp[0:C, 0:CAP], ACT.Copy).then_inc(e_xT, 1)
                act.wait_ge(e_up, 2 * e + 1)
                if e:
                    act.wait_ge(e_dn, e)
                ac.activation(h0[:, :], Cp[:, 0:CAP], ACT.Relu, bias=b1c[:, 2 * e:2 * e + 1]).then_inc(e_h0, 1)

        @block.tensor
        def _(pe):
            te_ = nc.tensor
            idn = ident[:, :]
            pe.wait_ge(w_in, 16 * 18)
            pe.wait_ge(pool_const, 4)
            te_.transpose(Bp[0:C, 256:384], wi[:, 1, :], idn)
            te_.transpose(Bp[:, 384:480], xbc3[:, :], ident[0:96, 0:96])
            te_.transpose(Bp[0:R, 512:640], dtw[:, :], idn)
            te_.transpose(Bp[:, 640:704], wo[:, :], ident[0:C, 0:C])
            te_.transpose(Bp[0:C, 704:768], pw[:, :], ident[0:C, 0:C])
            te_.transpose(Bp[:, 768:784], b1r[:, :], ident[0:2 * E, 0:2 * E])
            pe.wait_ge(taps_done, 1)
            te_.transpose(Bp[:, 0:128], taps[:, 0:2, :].rearrange("p k c -> p (k c)"), idn)
            te_.transpose(Bp[:, 128:256], taps[:, 2:4, :].rearrange("p k c -> p (k c)"), idn).then_inc(w_tr, 1)
            pe.wait_ge(w_ev, 1)
            te_.matmul(Cp[:, 0:P], xdt[:, :], dtwT[:, :], start=True, stop=True)
            te_.matmul(Cp[0:C + 1, HALF:HALF + C], gfold[:, :], pwT[:, :], start=True, stop=False)
            te_.matmul(Cp[0:C + 1, HALF:HALF + C], last1[:, :], pb[:, :], start=False, stop=True).then_inc(w_mm, 1)
            pe.wait_ge(w_ready, 1)

            def front(f, n):
                if n in (3, 4):
                    q = n - 3
                    pe.wait_ge(f_z, f + 1)
                    if q == 0 and not first(f):
                        pe.wait_ge(f_am, 2 * f)
                    if q == 1:
                        pe.wait_ge(f_top, 2 * f + 1)
                    for t in range(4):
                        ins = te_.transpose(M0[0:C + 1, t * P:(t + 1) * P], fz[:, 4 * q + t, :], idn)
                    ins.then_inc(f_tr, 1)
                if n in (5, 6):
                    q = n - 5
                    pe.wait_ge(f_bot, 2 * f + q + 1)
                    if q == 0:
                        pe.wait_ge(f_top, 2 * f + 2)
                    if q == 1:
                        pe.wait_ge(f_xcr, 2 * f + 1)
                    te_.matmul(M0[:, :], tapA[:, :], xnT[:, q * HALF:(q + 1) * HALF], start=True, stop=False)
                    te_.matmul(M0[:, :], tapB[:, :], xnT[:, 2 + q * HALF:2 + (q + 1) * HALF], start=False,
                               stop=True).then_inc(f_mx, 1)
                if n in (7, 8):
                    q = n - 7
                    pe.wait_ge((f_xcr, f_zr)[q], 2 * f + 2 - q)
                    te_.matmul(M0[:, :], wzT[:, :], xnT[0:C, 3 + q * HALF:3 + (q + 1) * HALF], start=True,
                               stop=True).then_inc(f_mz, 1)
                if n == 9:
                    pe.wait_ge(f_zr, 2 * f + 2)
                    for t in range(T):
                        ins = te_.matmul(M0[:, t * C:(t + 1) * C], xnT[0:C, 3 + t * P:3 + (t + 1) * P], skipI[:, :],
                                         start=True, stop=True)
                    ins.then_inc(f_sk, 1)
                if n in (10, 11):
                    q = n - 10
                    if q == 0:
                        pe.wait_ge(f_silu, f + 1)
                        pe.wait_ge(f_skx, f + 1)
                    else:
                        pe.wait_ge(f_r1, 2 * f + 1)
                    te_.matmul(M0[0:96, :], bcT[:, :], at_half(u, f, q), start=True, stop=True).then_inc(f_bc, 1)
                if n in (12, 13):
                    q = n - 12
                    pe.wait_ge((f_r1, f_am)[q], 2 * f + 2 - q)
                    te_.matmul(M0[:, :], wdt[:, :], at_half(u, f, q), start=True, stop=True).then_inc(f_dt, 1)

            def spread(dst, row, s, done):
                for q in range(2):
                    ins = te_.matmul(dst[:, HB[q]], sel[:, row, :], at_half(parts, s, q), start=True, stop=True)
                ins.then_inc(done, 1)

            def add_state(s, n):
                j = n // 2
                pe.wait_ge((s_pD, s_pP)[n % 2], 8 * s + j + 1)
                if n == 0 and not first(s):
                    pe.wait_ge(b_yt, s)
                for q in range(2):
                    ins = te_.matmul(Yp[:, HB[q]], idn, prod[:, 2 * (n % 2) + j % 2, HB[q]], start=(n == 0),
                                     stop=(n == 15), skip_group_check=True)
                ins.then_inc(s_sum, 1)

            def scan(s, n):
                j = n // 2
                if n < 15:
                    pe.wait_ge(s_scan, 16 * s + n + 1)
                    spread(Bp, n + 1, s, s_B)
                if n:
                    add_state(s, n - 1)
                if n < 15:
                    pe.wait_ge((s_pD, s_ccp)[n % 2], 8 * s + j + 1)
                    spread(Cp, N + n + 1, s, s_C)

            def back(g, n):
                if n == 1:
                    pe.wait_ge(b_yg, g + 1)
                    for t in range(T):
                        ins = te_.matmul(M1[:, t * C:(t + 1) * C], yt[:, t * P:(t + 1) * P], woT[:, :], start=True,
                                         stop=True)
                    ins.then_inc(b_op, 1)
                if n in (6, 7, 12, 13):
                    k, q = n // 8, (n - 6) % 2
                    if q == 0:
                        pe.wait_ge((b_n2, b_h3)[k], g + 1)
                        pe.wait_ge((b_y2, b_t1)[k], g + 1)
                    else:
                        pe.wait_ge((b_n2T, b_h3T)[k], 2 * g + 1)
                    src = (n2, rows)[k]
                    for t in range(4):
                        ins = te_.transpose(M1[0:C + 1, t * P:(t + 1) * P], src[:, 4 * q + t, 0:C + 1], idn)
                    ins.then_inc((b_tr, b_tr3)[k], 1)
                if n == 8:
                    pe.wait_ge(b_n2T, 2 * g + 2)
                    for t in range(T):
                        ins = te_.matmul(M1[:, t * C:(t + 1) * C], bT[:, t * P:(t + 1) * P], PW[:, :], start=True,
                                         stop=True)
                    ins.then_inc(b_pr, 1)
                if n == 14:
                    pe.wait_ge(late_in, 16 * 5)
                    pe.wait_ge(b_h3T, 2 * g + 2)
                    for t in range(T):
                        ins = te_.matmul(M1[:, t * E:(t + 1) * E], bT[:, t * P:(t + 1) * P], gw[:, :], start=True,
                                         stop=True)
                    ins.then_inc(b_gate, 1)
                if n == 16:
                    pe.wait_ge(b_oh, g + 1)
                    te_.matmul(M1[:, T * E:2 * T * E], tri[:, :], oh[:, :, 1:T + 1], start=True, stop=False,
                               skip_group_check=True)
                    te_.matmul(M1[:, T * E:2 * T * E], ones[:, :], before[:, :, 0:T], start=False, stop=True,
                               skip_group_check=True).then_inc(b_pos, 1)

            for n in range(17):
                front(0, n)
            pe.wait_ge(sel_done, 1)

            def step(s, has_front, has_back):
                pe.wait_ge(f_parts, 2 * s + 2)
                pe.wait_ge(f_mid, 2 * s + 2)
                if has_back:
                    pe.wait_ge(s_scan, 16 * s)
                spread(Bp, 0, s, s_B)
                if has_back:
                    pe.wait_ge(s_ccp, 8 * s)
                spread(Cp, N, s, s_C)
                if has_back:
                    add_state(s - 1, 15)
                for n in range(16):
                    scan(s, n)
                    if has_back:
                        back(s - 1, n)
                    if has_front:
                        front(s + 1, n)
                if has_back:
                    back(s - 1, 16)

            step(0, True, False)
            with pe.Fori(1, B - 1) as s:
                step(s, True, True)
            step(B - 1, False, True)
            add_state(B - 1, 15)
            for n in range(17):
                back(B - 1, n)

            def turn(e):
                pe.wait_ge(e_in[e % 3], 16 * (e // 3 + 1))
                if e:
                    pe.wait_ge(e_xT, e)
                for k in range(ET):
                    ins = te_.transpose(Bp[0:C, k * P:(k + 1) * P], xe[:, e % 3, k, 0:C], idn)
                ins.then_inc(e_tr, 1)

            cols = [slice(0, HALF), slice(HALF, CAP)]
            turn(0)
            for e in range(E):
                pe.wait_ge(e_xT, e + 1)
                for k, dst in enumerate((Cp, Yp)):
                    if e:
                        pe.wait_ge((e_h0, e_h1)[k], e)
                    for c in cols:
                        ins = te_.matmul(dst[:, c], w1s[:, e, k * P:(k + 1) * P], xT[:, c], start=True, stop=True)
                    ins.then_inc(e_up, 1)
                if e + 1 < E:
                    turn(e + 1)
                pe.wait_ge(e_h0, e + 1)
                pe.wait_ge(e_h1, e + 1)
                if e >= 2:
                    pe.wait_ge(e_yo, e - 1)
                for k in range(ET):
                    for i, hid in enumerate((h0, h1)):
                        ins = te_.matmul((M0, M1)[e % 2][:, k * C:(k + 1) * C], hid[:, k * P:(k + 1) * P],
                                         w2s[:, e, i, :], start=(i == 0), stop=(i == 1))
                ins.then_inc(e_dn, 1)

        @block.vector
        def _(dve):
            ve = nc.vector
            X = mybir.AxisListType.X
            dve.wait_ge(w_in, 16 * 18)
            for k in range(TAPS):
                ins = ve.tensor_scalar(taps[:, k, :], wi[:, 0, :], cw[:, k:k + 1], None, ALU.mult)
            ins.then_inc(taps_done, 1)
            dve.wait_ge(pool_const, 4)
            ve.tensor_scalar(gfold[:, 0:C], ident[0:C, 0:C], gcol[:, :], None, ALU.mult)
            ve.tensor_copy(gfold[:, C:C + 1], bcol[:, :])
            ve.tensor_scalar(skipI[:, :], ident[0:C, 0:C], skcol[:, :], None, ALU.mult)

            def front(f, n):
                if n == 0:
                    if first(f):
                        dve.wait_ge(x_first, 16)
                    else:
                        dve.wait_ge(x_rest, 16)
                        dve.wait_ge(f_z, f)
                    ve.reduce_sum(fs[:, 0, :], at_tiles(xs_in, f), X).then_inc(f_sum, 1)
                if n == 2:
                    dve.wait_ge(f_sq, f + 1)
                    ve.reduce_sum(fs[:, 2, :], fz[:, :, 0:C], X).then_inc(f_var, 1)
                if n in (3, 4):
                    q = n - 3
                    dve.wait_ge(f_top, 2 * f + q + 1)
                    if q == 0 and not first(f):
                        dve.wait_ge(f_dt, 2 * f)
                    ve.tensor_copy(xnT[C:P, 2 + q * HALF:2 + (q + 1) * HALF],
                                   xnT[0:C, 3 + q * HALF:3 + (q + 1) * HALF]).then_inc(f_bot, 1)
                if n in (10, 11):
                    q = n - 10
                    dve.wait_ge(f_hi, 2 * f + q + 1)
                    if q == 0 and not first(f):
                        dve.wait_ge(f_parts, 2 * f)
                    ve.tensor_tensor(r1[:, HB[q]], M0[0:96, :], at_half(parts, f, q), ALU.subtract).then_inc(f_r1, 1)
                    dve.wait_ge(f_r1, 2 * f + q + 1)
                    ve.tensor_copy(mid[:, HB[q]], r1[:, HB[q]]).then_inc(f_rest, 1)
                    dve.wait_ge(f_rest, 2 * f + q + 1)
                    ve.tensor_tensor(at_half(parts, f, q)[64:96], r1[64:96, HB[q]], mid[64:96, HB[q]],
                                     ALU.subtract).then_inc(f_parts, 1)
                if n == 15:
                    dve.wait_ge(f_exp, f + 1)
                    ve.tensor_scalar(at(du, f), te[:, :], 1.0, -1.0, ALU.add, ALU.add).then_inc(f_corr, 1)
                    dve.wait_ge(f_corr, 2 * f + 1)
                    dve.wait_ge(f_ln, f + 1)
                    ve.tensor_tensor(te[:, :], te[:, :], at(du, f), ALU.subtract).then_inc(f_corr, 1)
                    dve.wait_ge(f_corr, 2 * f + 2)
                    dve.wait_ge(f_lm, f + 1)
                    if not first(f):
                        dve.wait_ge(s_dA, 16 * f)
                    ve.tensor_tensor(delta[:, :], tabs[:, :], te[:, :], ALU.add).then_inc(f_delta, 1)
                    dve.wait_ge(f_delta, f + 1)
                    dve.wait_ge(f_silu, f + 1)
                    ve.tensor_tensor(at(du, f), delta[:, :], at(u, f), ALU.mult).then_inc(f_du, 1)

            def scan(s, n):
                j, own = n // 2, n % 2 == 0
                dve.wait_ge(s_B, 16 * s + n + 1)
                ve.tensor_tensor(Bp[:, :], Bp[:, :], at(du, s), ALU.mult).then_inc(s_mul, 1)
                dve.wait_ge(s_mul, 16 * s + n + 1)
                dve.wait_ge(s_dA, 16 * s + n + 1)
                hb = h[:, 2 * (n % 2) + j % 2, :]
                if not own and not (first(s) and j < 2):
                    dve.wait_ge(s_pP, 8 * s + j - 1)
                ve.tensor_tensor_scan(hb, dA[:, n % 3, :], Bp[:, :], 0.0, ALU.mult, ALU.add).then_inc(s_scan, 1)
                if own:
                    dve.wait_ge(s_scan, 16 * s + n + 1)
                    dve.wait_ge(s_C, 16 * s + n + 1)
                    if not (first(s) and j < 2):
                        dve.wait_ge(s_sum, 16 * s + n - 3)
                    ve.tensor_tensor(prod[:, j % 2, :], Cp[:, :], hb, ALU.mult).then_inc(s_pD, 1)

            def back(g, n):
                if n == 0:
                    dve.wait_ge(s_sum, 16 * g + 16)
                    ve.scalar_tensor_tensor(yt[:, :], at(u, g), Dcol[:, :], Yp[:, :], ALU.mult,
                                            ALU.add).then_inc(b_yt, 1)
                if n == 2:
                    dve.wait_ge(b_op, g + 1)
                    dve.wait_ge(f_skx, g + 1)
                    ve.tensor_tensor(y2[:, :, :], tiles(M1[:, :], C), at_tiles(skx, g), ALU.add).then_inc(b_y2, 1)
                    dve.wait_ge(b_y2, g + 1)
                    ve.reduce_sum(bs[:, 0, :], y2[:, :, :], X).then_inc(b_sum, 1)
                if n in (4, 10):
                    k = n // 8
                    dve.wait_ge((b_sq, b_sq3)[k], g + 1)
                    ve.reduce_sum(bs[:, 10 * k + 2, :], (n2, rows)[k][:, :, 0:C], X).then_inc((b_var, b_var3)[k], 1)
                if n == 8:
                    dve.wait_ge(b_pr, g + 1)
                    dve.wait_ge(b_sent, 16 + SENT * g)
                    t1 = rows[:, :, R_RES:R_RES + C]
                    ve.tensor_tensor(t1, tiles(M1[:, :], C), at_tiles(xs_in, g), ALU.add).then_inc(b_t1, 1)
                    dve.wait_ge(b_t1, g + 1)
                    ve.reduce_sum(bs[:, 10, :], t1, X).then_inc(b_sum3, 1)
                if n == 15:
                    link = Chain(dve, b_dve, g, 3)
                    lg = tiles(M1[:, 0:T * E], E)
                    dve.wait_ge(b_gate, g + 1)
                    link(ve.tensor_reduce(bs[:, 20, :], lg, X, ALU.max))
                    ve.tensor_tensor(ld[:, :, :], lg, over(bs[:, 20, :], E), ALU.subtract).then_inc(b_ld, 1)
                    dve.wait_ge(b_ld, g + 1)
                    link(ve.scalar_tensor_tensor(lrev[:, :, :], ld[:, :, :], 0.0, revc[:, :, :], ALU.is_equal,
                                                 ALU.mult))
                    link(ve.tensor_reduce(bs[:, 21, :], lrev[:, :, :], X, ALU.max))
                    link.end()
                    link = Chain(dve, b_dve2, g, 2)
                    link(ve.tensor_tensor(oh[:, :, 1:T + 1].rearrange("p e t -> p t e"), lrev[:, :, :],
                                          over(bs[:, 21, :], E), ALU.is_equal))
                    ve.tensor_tensor_scan(before[:, :, :].rearrange("p e t -> p (e t)"),
                                          resets[:, :, :].rearrange("p e t -> p (e t)"),
                                          oh[:, :, :].rearrange("p e t -> p (e t)"), 0.0, ALU.mult,
                                          ALU.add).then_inc(b_oh, 1)
                    dve.wait_ge(b_oh, g + 1)
                    link(ve.tensor_copy(oh[:, :, 0:1], before[:, :, T:T + 1]))
                    link.end()
                    dve.wait_ge(b_ex, g + 1)
                    link = Chain(dve, b_dve3, g, 7)
                    link(ve.reduce_sum(bs[:, 22, :], lex[:, :, :], X))
                    link(ve.reciprocal(rows[:, :, R_PRB:R_PRB + 1], bs[:, 22, :].unsqueeze(2)))
                    ve.tensor_copy(rows[:, :, R_ID:R_ID + 1].bitcast(I32), ids[:, bass.ds(g, 1), :].rearrange(
                        "p b t -> p t b"))
                    link(ve.tensor_scalar(bs[:, 23, :], bs[:, 21, :], -float(CAP), float(E * CAP), ALU.mult, ALU.add))
                    deferred[0] = link
                if n == 16:
                    link = deferred[0]
                    dve.wait_ge(b_pos, g + 1)
                    link(ve.tensor_tensor(lpo[:, :, :], M1[:, T * E:2 * T * E].rearrange("p (e t) -> p t e", e=E),
                                          oh[:, :, 1:T + 1].rearrange("p e t -> p t e"), ALU.mult))
                    link(ve.reduce_sum(bs[:, 24, :], lpo[:, :, :], X))
                    link(ve.tensor_scalar(bs[:, 25, :], bs[:, 24, :], float(CAP), float(2 * E * CAP), ALU.is_ge,
                                          ALU.mult))
                    link(ve.tensor_tensor(bs[:, 26, :], bs[:, 24, :], bs[:, 23, :], ALU.add))
                    link.end()
                    ve.tensor_tensor(chosen[:, :], bs[:, 26, :], bs[:, 25, :], ALU.add).then_inc(b_idx, 1)

            deferred = [None]
            dve.wait_ge(w_tr, 1)
            for dst, src in ((tapA[:, :], Bp[:, 0:128]), (tapB[:, :], Bp[:, 128:256]), (wzT[:, :], Bp[0:C, 256:384]),
                             (bcT[:, :], Bp[:, 384:480]), (dtwT[:, :], Bp[0:R, 512:640]), (woT[:, :], Bp[:, 640:704]),
                             (pwT[:, :], Bp[0:C, 704:768]), (b1c[:, :], Bp[:, 768:784])):
                ins = ve.tensor_copy(dst, src)
            ins.then_inc(w_ev, 1)
            dve.wait_ge(w_mm, 1)
            ve.tensor_copy(wdt[:, :], Cp[:, 0:P])
            ve.tensor_copy(PW[:, :], Cp[0:C + 1, HALF:HALF + C]).then_inc(w_ready, 1)
            dve.wait_ge(a_exp, 1)
            ve.tensor_scalar(aneg[:, :], aneg[:, :], -1.0, None, ALU.mult).then_inc(aneg_done, 1)
            for n in range(3):
                front(0, n)
            ve.tensor_copy(sel[:, :, :], sel1[:, :].unsqueeze(2).broadcast_to([96, 2 * N, P])).then_inc(sel_done, 1)
            for n in range(3, 17):
                front(0, n)

            def step(s, has_front, has_back):
                dve.wait_ge(f_du, s + 1)
                for n in range(16):
                    scan(s, n)
                    if has_back:
                        back(s - 1, n)
                    if has_front:
                        front(s + 1, n)
                if has_back:
                    back(s - 1, 16)

            step(0, True, False)
            with dve.Fori(1, B - 1) as s:
                step(s, True, True)
            step(B - 1, False, True)
            for n in range(17):
                back(B - 1, n)

            dve.wait_ge(late_in, 16 * 5)
            for e in range(E):
                dve.wait_ge(e_up, 2 * e + 2)
                if e:
                    dve.wait_ge(e_dn, e)
                ve.tensor_scalar(h1[:, :], Yp[:, 0:CAP], b1c[:, 2 * e + 1:2 * e + 2], 0.0, ALU.add,
                                 ALU.max).then_inc(e_h1, 1)
                link = Chain(dve, e_dve, e, 6)
                y, cl, ok, diff = (ye[:, i] for i in range(4))
                dve.wait_ge(e_dn, e + 1)
                link(ve.tensor_tensor(y, tiles((M0, M1)[e % 2][:, 0:ET * C], C, ET),
                                      b2s[:, e, :].unsqueeze(1).broadcast_to([P, ET, C]), ALU.add))
                link(ve.tensor_tensor(y, y, xe[:, e % 3, :, R_PRB:R_PRB + 1].broadcast_to([P, ET, C]), ALU.mult))
                ve.tensor_tensor(diff, y, y, ALU.subtract).then_inc(e_diff, 1)
                ve.tensor_scalar(cl, y, 1e4, -1e4, ALU.min, ALU.max)
                link(ve.tensor_tensor(ok, y, y, ALU.is_equal))
                dve.wait_ge(e_diff, e + 1)
                ve.tensor_scalar(fin[:, :, :], diff, 0.0, None, ALU.is_equal)
                link(ve.tensor_tensor(cl, cl, ok, ALU.mult))
                link(ve.copy_predicated(cl, fin[:, :, :], y))
                if e >= 2:
                    dve.wait_ge(e_out[(e - 2) % 3], 16 * ET * ((e - 2) // 3 + 1))
                ve.tensor_tensor(yo[:, e % 2], cl, xe[:, e % 3, :, R_RES:R_RES + C], ALU.add).then_inc(e_yo, 1)
                link(ve.tensor_copy(ok[:, 0:1, 0:1], cl[:, 0:1, 0:1]))
                link.end()


_INS = ['x', 'L0_conv_ln_g', 'L0_conv_ln_b', 'L0_conv_in_proj_w', 'L0_conv_conv_w', 'L0_conv_conv_b',
        'L0_conv_x_proj_w', 'L0_conv_dt_proj_w', 'L0_conv_dt_proj_b', 'L0_conv_A_log', 'L0_conv_D',
        'L0_conv_out_proj_w', 'L0_conv_proj_w', 'L0_conv_proj_b', 'L0_conv_skip_scale', 'L0_ffn_gate_w',
        'L0_ffn_gate_b', 'L0_ffn_w1', 'L0_ffn_b1', 'L0_ffn_w2', 'L0_ffn_b2']
_OUTS = [((4, 32, 32, 64), 'float32')]


def kernel(**inputs):
    import numpy as _np
    import concourse.bacc as _bacc
    from concourse import mybir as _mybir
    from concourse.bass_utils import run_bass_kernel_spmd as _run

    nc = _bacc.Bacc("TRN2", target_bir_lowering=False, num_devices=1)
    arrays, args = {}, []
    for name in _INS:
        a = _np.ascontiguousarray(inputs[name])
        arrays[f"in_{name}_dram"] = a
        args.append(nc.dram_tensor(f"in_{name}_dram", a.shape, _mybir.dt.from_np(a.dtype), kind="ExternalInput").ap())
    for i, (shape, dtype) in enumerate(_OUTS):
        dt = _mybir.dt.from_np(_np.dtype(dtype))
        args.append(nc.dram_tensor(f"out_{i}_dram", shape, dt, kind="ExternalOutput").ap())
    metaformer_layer(nc, *args)
    r = _run(nc, [arrays], core_ids=[0])
    got = tuple(r.results[0][f"out_{i}_dram"] for i in range(len(_OUTS)))
    return got[0]
```

```python
from contextlib import ExitStack

import concourse.bass as bass
from concourse import mybir

ALU = mybir.AluOpType
ACT = mybir.ActivationFunctionType
AX = mybir.AxisListType.X
F32 = mybir.dt.float32
BF16 = mybir.dt.bfloat16
I32 = mybir.dt.int32

P = 128
B, H, W, C = 4, 32, 32, 64
L = H * W
T = L // P
DI = 2 * C
N = 16
R = 4
TAPS = 4
HALF = 512
E, F = 8, 256
CAP = (B * L * 5 // 4 + E - 1) // E
ET = CAP // P
LN_C_EPS, LN_EPS = 1e-6, 1e-5

R_ONE, R_RES, R_PRB, R_ID, ROW = C, C + 1, 2 * C + 1, 2 * C + 2, 2 * C + 3
NOWHERE = 1 << 20
SENT = 16 * (T + 1)


class Chain:

    def __init__(self, eng, sem, turn, steps):
        self.eng, self.sem, self.base, self.steps, self.n = eng, sem, turn * steps, steps, 0

    def __call__(self, ins):
        self.n += 1
        assert self.n <= self.steps
        ins.then_inc(self.sem, 1)
        self.eng.wait_ge(self.sem, self.base + self.n)

    def end(self):
        assert self.n == self.steps, (self.n, self.steps)


def metaformer_layer(nc, x, ln_g, ln_b, in_proj_w, conv_w, conv_b, x_proj_w, dt_proj_w, dt_proj_b, A_log,
                     D, out_proj_w, proj_w, proj_b, skip_scale, gate_w, gate_b, w1, b1, w2, b2, out):
    x_dram = x.rearrange("b h w c -> (b h w) c").rearrange("(b t p) c -> b p t c", b=B, p=P)
    out_rows = out.rearrange("b h w c -> (b h w) c")
    out_dram = out_rows.rearrange("(b t p) c -> b p t c", b=B, p=P)
    slots_dram = nc.dram_tensor("slots", (E * CAP, ROW), F32, kind="Internal").ap()

    with ExitStack() as ctx:
        def sb(name, shape, dt=F32):
            return ctx.enter_context(nc.sbuf_tensor(name, shape, dt))

        def sem(name):
            return ctx.enter_context(nc.semaphore(name))

        Bp = ctx.enter_context(nc.psum_tensor("Bp", [P, L], F32))
        Cp = ctx.enter_context(nc.psum_tensor("Cp", [P, L], F32))
        Yp = ctx.enter_context(nc.psum_tensor("Yp", [P, L], F32))
        M0 = ctx.enter_context(nc.psum_tensor("M0", [P, HALF], F32))
        M1 = ctx.enter_context(nc.psum_tensor("M1", [P, HALF], F32))

        ident = sb("ident", [P, P])
        sel1 = sb("sel1", [96, 2 * N], BF16)
        sel = sb("sel", [96, 2 * N, P], BF16)
        tri = sb("tri", [P, P], BF16)
        ones = sb("ones", [P, P], BF16)
        revc = sb("revc", [P, T, E])
        revi = sb("revi", [P, T, E], I32)
        ids = sb("ids", [P, B, T], I32)
        resets = sb("resets", [P, E, T + 1])
        mhalf = sb("mhalf", [P, B * T])
        invC = sb("invC", [P, B * T])
        zero = sb("zero", [P, T], I32)
        in_scale = sb("in_scale", [P, B * T])
        in_eps = sb("in_eps", [P, B * T])
        eps5 = sb("eps5", [P, T])
        gcol = sb("gcol", [C, 1])
        bcol = sb("bcol", [C, 1])
        cw = sb("cw", [P, TAPS])
        cb = sb("cb", [P, 1])
        xbc = sb("xbc", [2 * N, P])
        xdt = sb("xdt", [R, P])
        dtw = sb("dtw", [P, R])
        dtb = sb("dtb", [P, 1])
        alog = sb("alog", [P, N])
        aneg = sb("aneg", [P, N])
        Dcol = sb("Dcol", [P, 1])
        wo = sb("wo", [C, P])
        pw = sb("pw", [C, C])
        pb = sb("pb", [1, C])
        last1 = sb("last1", [1, C + 1])
        gfold = sb("gfold", [C, C + 1])
        skcol = sb("skcol", [C, 1])
        skipI = sb("skipI", [C, C])
        gw = sb("gw", [C + 1, E])
        w1s = sb("w1s", [C, E, F])
        w2s = sb("w2s", [P, E, 2, C])
        b1r = sb("b1r", [2 * E, P])
        b1c = sb("b1c", [P, 2 * E])
        b2s = sb("b2s", [P, E, C])
        tapA = sb("tapA", [P, P])
        tapB = sb("tapB", [P, P])
        wzT = sb("wzT", [C, P])
        bcT = sb("bcT", [P, 2 * N])
        identb = sb("identb", [P, P], BF16)
        dtwT = sb("dtwT", [R, P])
        woT = sb("woT", [P, C])
        pwT = sb("pwT", [C, C])
        wdt = sb("wdt", [P, P])
        PW = sb("PW", [C + 1, C])

        xs_in = sb("xs_in", [P, B, T, C])
        u = sb("u", [P, B, L])
        sz = sb("sz", [P, B, L])
        delta = sb("delta", [P, L])
        du = sb("du", [P, B, L])
        parts = sb("parts", [96, B, L], BF16)

        fs = sb("fs", [P, 6, B * T])
        fz = sb("fz", [P, B, T, C])
        skx = fz
        zt = sb("zt", [P, T, C + 1])
        xnT = sb("xnT", [P, L + 3])
        rest = sb("rest", [P, T, 2 * N])
        bc = sb("bc", [P, T, 3, 2 * N], BF16)
        big = sb("big", [P, L], mybir.dt.uint8)
        tabs = sb("tabs", [P, L])
        trel = sb("trel", [P, L])
        te = sb("te", [P, L])
        dA = sb("dA", [P, 3, L])
        h = sb("h", [P, 4, L])
        prod = sb("prod", [P, 4, L])
        csb = sb("csb", [P, 2, L])
        yt = sb("yt", [P, L])
        yt_free = yt
        bs = sb("bs", [P, 28, T])
        y2 = sb("y2", [P, T, C])
        bxm = sb("bxm", [P, T, C])
        n2 = sb("n2", [P, T, C + 1])
        bT = sb("bT", [C + 1, L])
        rows = sb("rows", [P, T, ROW])
        ld = sb("ld", [P, T, E])
        lex = sb("lex", [P, T, E])
        lrev = sb("lrev", [P, T, E])
        lpo = sb("lpo", [P, T, E])
        oh = sb("oh", [P, E, T + 1], BF16)
        before = sb("before", [P, E, T + 1], BF16)
        chosen = sb("chosen", [P, T], I32)
        slot = sb("slot", [P, T], I32)
        fill = sb("fill", [P, ROW])
        def within(buf, start, *dims):
            size = 1
            for d in dims:
                size *= d
            flat = buf[:, :, :].rearrange("p a l -> p (a l)")[:, start:start + size]
            names = "abcd"[:len(dims)]
            if len(dims) == 1:
                return flat
            return flat.rearrange(f"p ({' '.join(names)}) -> p {' '.join(names)}",
                                  **{k: d for k, d in zip(names[1:], dims[1:])})

        wi = within(dA, 0, 2, C)
        taps = within(dA, L, TAPS, C)
        squares = within(prod, 0, B * T, C)
        xe = within(h, 0, 3, ET, ROW)
        xT = within(prod, 0, CAP)[0:C]
        h0 = within(prod, L, CAP)
        h1 = within(prod, 2 * L, CAP)
        ye = within(dA, 0, 4, ET, C)
        yo = within(prod, 3 * L, 2, ET, C)
        fin = within(dA, 2 * L, ET, C).bitcast(I32)

        x_first, x_rest = sem("x_first"), sem("x_rest")
        w_in, late_in = sem("w_in"), sem("late_in")
        pool_const, pool_init = sem("pool_const"), sem("pool_init")
        sel_done, taps_done = sem("sel_done"), sem("taps_done")
        w_tr, w_ev, w_mm, w_ready, aneg_done, a_exp = (sem("w_tr"), sem("w_ev"), sem("w_mm"), sem("w_ready"),
                                                       sem("aneg_done"), sem("a_exp"))
        n_sum, n_mean, n_xm, n_sq, n_var, n_rstd, n_z = map(sem, "n_sum n_mean n_xm n_sq n_var n_rstd n_z".split())
        (f_z, f_tr, f_top, f_bot, f_mx, f_xcr, f_mz, f_zr, f_silu, f_sk, f_skx, f_bc, f_hi, f_rest, f_mid, f_lo, f_btr,
         f_parts, f_dt, f_am, f_exp, f_ln, f_lost, f_corr, f_big, f_log, f_delta, f_du) = map(sem, (
             "f_z f_tr f_top f_bot f_mx f_xcr f_mz f_zr f_silu f_sk f_skx f_bc f_hi f_rest f_mid f_lo f_btr "
             "f_parts f_dt f_am f_exp f_ln f_lost f_corr f_big f_log f_delta f_du").split())
        s_B, s_mul, s_dA, s_scan, s_C, s_ccp, s_pD, s_pP, s_sum = map(sem, (
            "s_B s_mul s_dA s_scan s_C s_ccp s_pD s_pP s_sum").split())
        (b_yt, b_yg, b_op, b_y2, b_sum, b_xm, b_sq, b_var, b_n2, b_tr, b_n2T, b_pr, b_t1, b_sum3, b_xm3, b_sq3,
         b_var3, b_h3, b_tr3, b_h3T, b_gate, b_ld, b_ex, b_oh, b_pos, b_idx, b_pool, b_dve, b_dve2, b_dve3, b_sent) = map(sem, (
             "b_yt b_yg b_op b_y2 b_sum b_xm b_sq b_var b_n2 b_tr b_n2T b_pr b_t1 b_sum3 b_xm3 b_sq3 "
             "b_var3 b_h3 b_tr3 b_h3T b_gate b_ld b_ex b_oh b_pos b_idx b_pool b_dve b_dve2 b_dve3 b_sent").split())
        fill_done = sem("fill_done")
        e_in = [sem(f"e_in{i}") for i in range(3)]
        e_out = [sem(f"e_out{i}") for i in range(3)]
        e_tr, e_xT, e_up, e_h0, e_h1, e_dn, e_yo, e_dve, e_diff = map(sem, (
            "e_tr e_xT e_up e_h0 e_h1 e_dn e_yo e_dve e_diff").split())

        def at(buf, b):
            return buf[:, bass.ds(b, 1), :].rearrange("p b l -> p (b l)")

        def at_half(buf, b, q):
            return buf[:, bass.ds(b, 1), q * HALF:(q + 1) * HALF].rearrange("p b l -> p (b l)")

        def at_tiles(buf, b):
            return buf[:, bass.ds(b, 1), :, :].rearrange("p b t c -> p (b t) c")

        def over(col, n):
            return col.unsqueeze(2).broadcast_to([P, col.shape[1], n])

        def first(b):
            return isinstance(b, int) and b == 0

        def tiles(psum, n, k=T):
            return psum.rearrange("p (t c) -> p t c", t=k)[:, :, 0:n]

        block = ctx.enter_context(nc.Block())
        HB = [slice(0, HALF), slice(HALF, L)]
        M0b = M0[:, :].bitcast(BF16)
        bc_psum = M0[:, 0:T * 2 * N].rearrange("p (t r) -> p t r", t=T)

        @block.sync
        def _(sp):
            sp.dma_start(xs_in[:, 0], x_dram[0]).then_inc(x_first, 16)
            for dst, src in ((wi[:, :, :], in_proj_w.rearrange("(h p) c -> p h c", p=P)),
                             (cw[:, :], conv_w),
                             (gcol[:, :], ln_g.unsqueeze(1)), (bcol[:, :], ln_b.unsqueeze(1)),
                             (cb[:, :], conv_b.unsqueeze(1)), (dtb[:, :], dt_proj_b.unsqueeze(1)),
                             (xbc[:, :], x_proj_w[R:R + 2 * N, :]), (xdt[:, :], x_proj_w[0:R, :]),
                             (dtw[:, :], dt_proj_w), (alog[:, :], A_log), (Dcol[:, :], D.unsqueeze(1)),
                             (wo[:, :], out_proj_w), (pw[:, :], proj_w), (pb[:, :], proj_b.unsqueeze(0)),
                             (skcol[:, :], skip_scale.unsqueeze(0).broadcast_to([C, 1])),
                             (b1r[:, :], b1.rearrange("e (h f) -> (e h) f", h=2))):
                sp.dma_start(dst, src).then_inc(w_in, 16)
            sp.dma_start(xs_in[:, 1:B], x_dram[1:B].rearrange("b p t c -> p b t c")).then_inc(x_rest, 16)
            for dst, src in ((gw[0:C, :], gate_w), (gw[C:C + 1, :], gate_b.unsqueeze(0)),
                             (w1s[:, :, :], w1.rearrange("e c f -> c e f")),
                             (w2s[:, :, :, :], w2.rearrange("e (h f) c -> f e h c", h=2)),
                             (b2s[:, :, :], b2.unsqueeze(0).broadcast_to([P, E, C]))):
                sp.dma_start(dst, src).then_inc(late_in, 16)
            sp.wait_ge(b_sent, 16 + SENT * B)
            for e in range(E):
                if e >= 3:
                    sp.wait_ge(e_out[e % 3], 16 * ET * (e // 3))
                sp.dma_start(xe[:, e % 3],
                             slots_dram[e * CAP:(e + 1) * CAP, :].rearrange("(k p) r -> p k r", p=P)
                             ).then_inc(e_in[e % 3], 16)

        @block.gpsimd
        def _(pool):
            po = nc.gpsimd
            po.memset(ident[:, :], 0.0).then_inc(pool_init, 1)
            po.memset(sel1[:, :], 0.0).then_inc(pool_init, 1)
            po.memset(tri[:, :], 1.0).then_inc(pool_init, 1)
            po.memset(ones[:, :], 1.0)
            po.memset(mhalf[:, :], -0.5)
            po.memset(invC[:, :], 1.0 / C)
            po.memset(zero[:, :], 0)
            po.memset(in_scale[:, :], (1.0 + LN_EPS) / C)
            po.memset(in_eps[:, :], LN_C_EPS * LN_EPS)
            po.memset(eps5[:, :], LN_EPS)
            po.memset(resets[:, :, :], 1.0)
            po.memset(last1[:, :], 0.0)
            po.memset(n2[:, :, C:C + 1], 1.0)
            po.memset(zt[:, :, C:C + 1], 1.0)
            po.memset(rows[:, :, R_ONE:R_ONE + 1], 1.0)
            po.memset(xnT[:, 0:3], 0.0)
            po.memset(oh[:, :, 0:1], 0.0)
            po.memset(fill[:, :], 0.0).then_inc(fill_done, 1)
            po.iota(revi[:, :, :], pattern=[[0, T], [-1, E]], base=E, channel_multiplier=0)
            po.iota(ids[:, :, :], pattern=[[L, B], [P, T]], base=0, channel_multiplier=1).then_inc(pool_init, 1)
            pool.wait_ge(pool_init, 4)
            pool.wait_ge(fill_done, 1)
            po.affine_select(out=ident[:, :], in_=ident[:, :], compare_op=ALU.not_equal, fill=1.0, base=0,
                             pattern=[[-1, P]], channel_multiplier=1)
            po.iota(fill[:, R_ID:R_ID + 1].bitcast(I32), pattern=[[0, 1]], base=NOWHERE,
                    channel_multiplier=0).then_inc(fill_done, 1)
            po.affine_select(out=tri[:, :], in_=tri[:, :], compare_op=ALU.is_gt, fill=0.0, base=0,
                             pattern=[[1, P]], channel_multiplier=-1)
            po.memset(resets[:, :, 0:1], 0.0)
            po.memset(last1[:, C:C + 1], 1.0)
            for k in range(3):
                po.affine_select(out=sel1[:, :], in_=sel1[:, :], compare_op=ALU.not_equal, fill=1.0, base=-32 * k,
                                 pattern=[[-1, 2 * N]], channel_multiplier=1).then_inc(pool_const, 1)
                pool.wait_ge(pool_const, k + 1)
            po.tensor_copy(revc[:, :, :], revi[:, :, :]).then_inc(pool_const, 1)
            pool.wait_ge(pool_const, 4)
            pool.wait_ge(fill_done, 2)
            po.dma_start(slots_dram.rearrange("(k p) r -> p k r", p=P),
                         fill[:, :].unsqueeze(1).broadcast_to([P, E * ET, ROW])).then_inc(b_sent, 16)

            def rstd(link, s, var_sum, o):
                link(po.tensor_tensor(s[:, o, :], s[:, var_sum, :], invC[:, 0:T], ALU.mult))
                link(po.tensor_tensor(s[:, o + 1, :], s[:, o, :], eps5[:, :], ALU.add))
                link(po.tensor_tensor(s[:, o + 2, :], s[:, o + 1, :], mhalf[:, 0:T], ALU.pow))

            def input_norm(k, b0, b1):
                c, m = slice(b0 * T, b1 * T), (b1 - b0) * T
                z, xin = (buf[:, b0:b1].rearrange("p b t c -> p (b t) c") for buf in (fz, xs_in))
                pool.wait_ge(n_sum, k + 1)
                po.tensor_tensor(fs[:, 1, c], fs[:, 0, c], invC[:, 0:m], ALU.mult).then_inc(n_mean, 1)
                pool.wait_ge(n_mean, k + 1)
                po.tensor_tensor(z, xin, over(fs[:, 1, c], C), ALU.subtract).then_inc(n_xm, 1)
                pool.wait_ge(n_var, k + 1)
                link = Chain(pool, n_rstd, k, 3)
                link(po.tensor_tensor(fs[:, 3, c], fs[:, 2, c], in_scale[:, 0:m], ALU.mult))
                link(po.tensor_tensor(fs[:, 4, c], fs[:, 3, c], in_eps[:, 0:m], ALU.add))
                link(po.tensor_tensor(fs[:, 5, c], fs[:, 4, c], mhalf[:, 0:m], ALU.pow))
                link.end()
                po.tensor_tensor(z, z, over(fs[:, 5, c], C), ALU.mult).then_inc(n_z, 1)

            def scan(s, n):
                j = n // 2
                pool.wait_ge(s_ccp, 8 * s + j + 1)
                pool.wait_ge(s_scan, 16 * s + n + 1)
                if not (first(s) and j < 2):
                    pool.wait_ge(s_sum, 16 * s + n - 3)
                po.tensor_tensor(prod[:, 2 + j % 2, :], h[:, 2 + j % 2, :], csb[:, j % 2, :],
                                 ALU.mult).then_inc(s_pP, 1)

            def front(f, n):
                if n == 13:
                    pool.wait_ge(f_ln, f + 1)
                    po.tensor_tensor(yt_free[:, :], te[:, :], yt_free[:, :], ALU.subtract).then_inc(f_lost, 1)
                    pool.wait_ge(f_lost, f + 1)
                    po.tensor_tensor(tabs[:, :], tabs[:, :], yt_free[:, :], ALU.add).then_inc(f_corr, 1)

            def back(g, n):
                if n in (3, 8):
                    k = 0 if n == 3 else 1
                    pool.wait_ge((b_sum, b_sum3)[k], g + 1)
                    o = 10 * k
                    link = Chain(pool, b_pool, 2 * g + k, 4)
                    link(po.tensor_tensor(bs[:, o + 1, :], bs[:, o, :], invC[:, 0:T], ALU.mult))
                    src = (y2[:, :, :], rows[:, :, R_RES:R_RES + C])[k]
                    po.tensor_tensor(bxm[:, :, :], src, over(bs[:, o + 1, :], C),
                                     ALU.subtract).then_inc((b_xm, b_xm3)[k], 1)
                    links[k] = link
                if n in (4, 9):
                    k = 0 if n == 4 else 1
                    o = 10 * k
                    pool.wait_ge((b_var, b_var3)[k], g + 1)
                    link = links[k]
                    rstd(link, bs, o + 2, o + 3)
                    link.end()
                    dst = (n2[:, :, 0:C], rows[:, :, 0:C])[k]
                    po.tensor_tensor(dst, bxm[:, :, :], over(bs[:, o + 5, :], C),
                                     ALU.mult).then_inc((b_n2, b_h3)[k], 1)
                if n == 15:
                    pool.wait_ge(b_idx, g + 1)
                    po.tensor_tensor(slot[:, :], chosen[:, :], zero[:, :], ALU.add)
                    pool.drain()
                    po.dma_start(out_dram[bass.ds(g, 1)].rearrange("b p t c -> p (b t) c"),
                                 rows[:, :, R_RES:R_RES + C]).then_inc(b_sent, 16)
                if n in (15, 16):
                    for t in range(0, 2) if n == 15 else range(2, T):
                        po.indirect_dma_start(slots_dram[:, :], bass.IndirectOffsetOnAxis(ap=slot[:, t:t + 1], axis=0),
                                              rows[:, t, :], None, bounds_check=last_slot,
                                              oob_is_err=False).then_inc(b_sent, 16)

            links = [None, None]
            last_slot = po.to_reg(E * CAP - 1)
            input_norm(0, 0, 1)
            input_norm(1, 1, B)

            front(0, 13)

            def step(s, has_front, has_back):
                for n in range(16):
                    if has_back:
                        back(s - 1, n)
                    if has_front:
                        front(s + 1, n)
                    if n % 2:
                        scan(s, n)
                if has_back:
                    back(s - 1, 16)

            step(0, True, False)
            with pool.Fori(1, B - 1) as s:
                step(s, True, True)
            step(B - 1, False, True)
            for n in range(17):
                back(B - 1, n)
            pool.wait_ge(b_sent, 16 + SENT * B)
            for e in range(E):
                pool.wait_ge(e_yo, e + 1)
                for k in range(ET):
                    po.indirect_dma_start(out_rows, bass.IndirectOffsetOnAxis(
                        ap=xe[:, e % 3, k, R_ID:R_ID + 1].bitcast(I32), axis=0), yo[:, e % 2, k, :], None,
                        bounds_check=B * L - 1, oob_is_err=False).then_inc(e_out[e % 3], 16)
            for i in range(3):
                pool.wait_ge(e_out[i], 16 * ET * len(range(i, E, 3)))

        @block.scalar
        def _(act):
            ac = nc.scalar

            def act_set():
                ac.preload_act_table_set("natural_log_exp_and_others")

            def front(f, n):
                if n in (1, 2):
                    q = n - 1
                    act.wait_ge(f_tr, 2 * f + q + 1)
                    ac.activation(xnT[0:C, 3 + q * HALF:3 + (q + 1) * HALF], M0[0:C, :], ACT.Identity,
                                  bias=bcol[:, :], scale=gcol[:, :]).then_inc(f_top, 1)
                if n in (4, 5):
                    q = n - 4
                    act.wait_ge(f_mx, 2 * f + q + 1)
                    ac.activation(at_half(u, f, q), M0[:, :], ACT.Identity, bias=cb[:, :]).then_inc(f_xcr, 1)
                if n in (6, 7):
                    q = n - 6
                    act.wait_ge(f_mz, 2 * f + q + 1)
                    ac.activation(at_half(sz, f, q), M0[:, :], ACT.Copy).then_inc(f_zr, 1)
                if n == 7:
                    act.drain()
                    ac.activation(yt_free[:, :], at(u, f), ACT.Silu)
                    ac.activation(at(u, f), at(u, f), ACT.Silu)
                    ac.activation(at(sz, f), at(sz, f), ACT.Silu).then_inc(f_silu, 1)
                    act_set()
                if n == 8:
                    act.wait_ge(f_sk, f + 1)
                    ac.activation(at_tiles(skx, f), tiles(M0[:, :], C), ACT.Copy).then_inc(f_skx, 1)
                if n in (10, 11):
                    q = n - 10
                    act.wait_ge(f_dt, 2 * f + q + 1)
                    ac.activation(tabs[:, HB[q]], M0[:, :], ACT.Abs, bias=dtb[:, :])
                    ac.activation(trel[:, HB[q]], M0[:, :], ACT.Relu, bias=dtb[:, :]).then_inc(f_am, 1)
                if n == 11:
                    act.drain()
                    ac.activation(te[:, :], tabs[:, :], ACT.Exp, scale=-1.0).then_inc(f_exp, 1)
                    act.drain()
                    ac.activation(at(du, f), te[:, :], ACT.Square, scale=0.5 ** 0.5)
                if n == 12:
                    act.wait_ge(f_bc, f + 1)
                    ac.activation(bc[:, :, 0, :], bc_psum, ACT.Copy).then_inc(f_hi, 1)
                    ac.activation(yt_free[:, :], te[:, :], ACT.Copy, bias=1.0)
                    act.drain()
                    ac.activation(tabs[:, :], yt_free[:, :], ACT.Ln)
                    ac.activation(yt_free[:, :], yt_free[:, :], ACT.Copy, bias=-1.0).then_inc(f_ln, 1)
                if n == 14:
                    act.wait_ge(f_btr, f + 1)
                    ac.activation(at(parts, f), M0b[0:96, :], ACT.Copy).then_inc(f_parts, 1)

            def decay(s, n):
                if not (first(s) and n < 3):
                    act.wait_ge(s_scan, 16 * s + n - 2)
                ac.activation(dA[:, n % 3, :], delta[:, :], ACT.Exp, scale=aneg[:, n:n + 1]).then_inc(s_dA, 1)

            def scan(s, n):
                if n + 2 < 16:
                    decay(s, n + 2)
                if n % 2:
                    j = n // 2
                    act.wait_ge(s_C, 16 * s + n + 1)
                    if not (first(s) and j < 2):
                        act.wait_ge(s_pP, 8 * s + j - 1)
                    ac.activation(csb[:, j % 2, :], Cp[:, :], ACT.Copy).then_inc(s_ccp, 1)

            def back(g, n):
                if n in (3, 8):
                    k = n // 8
                    act.wait_ge((b_xm, b_xm3)[k], g + 1)
                    ac.activation((n2, rows)[k][:, :, 0:C], bxm[:, :, :], ACT.Square).then_inc((b_sq, b_sq3)[k], 1)
                if n in (5, 6, 10, 11):
                    k, q = n // 10, n % 5 if n < 10 else n - 10
                    act.wait_ge((b_tr, b_tr3)[k], 2 * g + q + 1)
                    ac.activation(bT[:, HB[q]], M1[0:C + 1, :], ACT.Copy).then_inc((b_n2T, b_h3T)[k], 1)
                if n == 13:
                    act.wait_ge(b_ld, g + 1)
                    ac.activation(lex[:, :, :], ld[:, :, :], ACT.Exp).then_inc(b_ex, 1)

            act_set()
            act.wait_ge(w_in, 16 * 16)
            ac.activation(aneg[:, :], alog[:, :], ACT.Exp).then_inc(a_exp, 1)

            def input_norm(k, b0, b1):
                act.wait_ge(n_xm, k + 1)
                ac.activation(squares[:, b0 * T:b1 * T, :], fz[:, b0:b1].rearrange("p b t c -> p (b t) c"),
                              ACT.Square).then_inc(n_sq, 1)

            input_norm(0, 0, 1)
            for n in range(17):
                front(0, n)
                if n == 2:
                    input_norm(1, 1, B)
            act.wait_ge(aneg_done, 1)

            def step(s, has_front, has_back):
                act.wait_ge(f_delta, s + 1)
                decay(s, 0)
                decay(s, 1)
                for n in range(16):
                    scan(s, n)
                    if has_back:
                        back(s - 1, n)
                    if has_front:
                        front(s + 1, n)

            step(0, True, False)
            with act.Fori(1, B - 1) as s:
                step(s, True, True)
            step(B - 1, False, True)
            for n in range(17):
                back(B - 1, n)
            for e in range(E):
                act.wait_ge(e_tr, e + 1)
                if e:
                    act.wait_ge(e_up, 2 * e)
                ac.activation(xT[:, :], Bp[0:C, 0:CAP], ACT.Copy).then_inc(e_xT, 1)
                act.wait_ge(e_up, 2 * e + 1)
                if e:
                    act.wait_ge(e_dn, e)
                ac.activation(h0[:, :], Cp[:, 0:CAP], ACT.Relu, bias=b1c[:, 2 * e:2 * e + 1]).then_inc(e_h0, 1)

        @block.tensor
        def _(pe):
            te_ = nc.tensor
            idn = ident[:, :]
            pe.wait_ge(w_in, 16 * 16)
            pe.wait_ge(pool_const, 4)
            te_.transpose(Bp[0:C, 256:384], wi[:, 1, :], idn)
            te_.transpose(Bp[:, 384:416], xbc[:, :], ident[0:2 * N, 0:2 * N])
            te_.transpose(Bp[0:R, 512:640], dtw[:, :], idn)
            te_.transpose(Bp[:, 640:704], wo[:, :], ident[0:C, 0:C])
            te_.transpose(Bp[0:C, 704:768], pw[:, :], ident[0:C, 0:C])
            te_.transpose(Bp[:, 768:784], b1r[:, :], ident[0:2 * E, 0:2 * E])
            pe.wait_ge(taps_done, 1)
            te_.transpose(Bp[:, 0:128], taps[:, 0:2, :].rearrange("p k c -> p (k c)"), idn)
            te_.transpose(Bp[:, 128:256], taps[:, 2:4, :].rearrange("p k c -> p (k c)"), idn).then_inc(w_tr, 1)
            pe.wait_ge(w_ev, 1)
            te_.matmul(Cp[:, 0:P], xdt[:, :], dtwT[:, :], start=True, stop=True)
            te_.matmul(Cp[0:C + 1, HALF:HALF + C], gfold[:, :], pwT[:, :], start=True, stop=False)
            te_.matmul(Cp[0:C + 1, HALF:HALF + C], last1[:, :], pb[:, :], start=False, stop=True).then_inc(w_mm, 1)
            pe.wait_ge(w_ready, 1)

            def front(f, n):
                if n in (0, 1):
                    q = n
                    if q == 0:
                        pe.wait_ge(f_z, f + 1)
                        if not first(f):
                            pe.wait_ge(f_parts, f)
                    else:
                        pe.wait_ge(f_top, 2 * f + 1)
                    for t in range(4):
                        ins = te_.transpose(M0[0:C + 1, t * P:(t + 1) * P], zt[:, 4 * q + t, :], idn)
                    ins.then_inc(f_tr, 1)
                if n in (3, 4):
                    q = n - 3
                    pe.wait_ge(f_bot, 2 * f + q + 1)
                    if q == 0:
                        pe.wait_ge(f_top, 2 * f + 2)
                    if q == 1:
                        pe.wait_ge(f_xcr, 2 * f + 1)
                    te_.matmul(M0[:, :], tapA[:, :], xnT[:, q * HALF:(q + 1) * HALF], start=True, stop=False)
                    te_.matmul(M0[:, :], tapB[:, :], xnT[:, 2 + q * HALF:2 + (q + 1) * HALF], start=False,
                               stop=True).then_inc(f_mx, 1)
                if n in (5, 6):
                    q = n - 5
                    pe.wait_ge((f_xcr, f_zr)[q], 2 * f + 2 - q)
                    te_.matmul(M0[:, :], wzT[:, :], xnT[0:C, 3 + q * HALF:3 + (q + 1) * HALF], start=True,
                               stop=True).then_inc(f_mz, 1)
                if n == 7:
                    pe.wait_ge(f_zr, 2 * f + 2)
                    for t in range(T):
                        ins = te_.matmul(M0[:, t * C:(t + 1) * C], xnT[0:C, 3 + t * P:3 + (t + 1) * P], skipI[:, :],
                                         start=True, stop=True)
                    ins.then_inc(f_sk, 1)
                if n in (9, 10):
                    q = n - 9
                    if q == 0:
                        pe.wait_ge(f_silu, f + 1)
                        pe.wait_ge(f_skx, f + 1)
                    else:
                        pe.wait_ge(f_am, 2 * f + 1)
                    te_.matmul(M0[:, :], wdt[:, :], at_half(u, f, q), start=True, stop=True).then_inc(f_dt, 1)
                if n == 11:
                    pe.wait_ge(f_am, 2 * f + 2)
                    for t in range(T):
                        ins = te_.matmul(M0[:, t * 2 * N:(t + 1) * 2 * N], yt_free[:, t * P:(t + 1) * P], bcT[:, :],
                                         start=True, stop=True)
                    ins.then_inc(f_bc, 1)
                if n == 13:
                    pe.wait_ge(f_lo, f + 1)
                    for t in range(T):
                        ins = te_.transpose(M0b[0:96, t * P:(t + 1) * P],
                                            bc[:, t, :, :].rearrange("p k r -> p (k r)"), identb[:, :])
                    ins.then_inc(f_btr, 1)

            def spread(dst, row, s, done):
                for q in range(2):
                    ins = te_.matmul(dst[:, HB[q]], sel[:, row, :], at_half(parts, s, q), start=True, stop=True)
                ins.then_inc(done, 1)

            def add_state(s, n):
                j = n // 2
                pe.wait_ge((s_pD, s_pP)[n % 2], 8 * s + j + 1)
                if n == 0 and not first(s):
                    pe.wait_ge(b_yt, s)
                for q in range(2):
                    ins = te_.matmul(Yp[:, HB[q]], idn, prod[:, 2 * (n % 2) + j % 2, HB[q]], start=(n == 0),
                                     stop=(n == 15), skip_group_check=True)
                ins.then_inc(s_sum, 1)

            def scan(s, n):
                j = n // 2
                if n < 15:
                    pe.wait_ge(s_scan, 16 * s + n + 1)
                    spread(Bp, n + 1, s, s_B)
                if n:
                    add_state(s, n - 1)
                if n < 15:
                    pe.wait_ge((s_pD, s_ccp)[n % 2], 8 * s + j + 1)
                    spread(Cp, N + n + 1, s, s_C)

            def back(g, n):
                if n == 1:
                    pe.wait_ge(b_yg, g + 1)
                    for t in range(T):
                        ins = te_.matmul(M1[:, t * C:(t + 1) * C], yt[:, t * P:(t + 1) * P], woT[:, :], start=True,
                                         stop=True)
                    ins.then_inc(b_op, 1)
                if n in (4, 5, 9, 10):
                    k, q = n // 9, (n - 4) % 5
                    if q == 0:
                        pe.wait_ge((b_n2, b_h3)[k], g + 1)
                        pe.wait_ge((b_y2, b_t1)[k], g + 1)
                    else:
                        pe.wait_ge((b_n2T, b_h3T)[k], 2 * g + 1)
                    src = (n2, rows)[k]
                    for t in range(4):
                        ins = te_.transpose(M1[0:C + 1, t * P:(t + 1) * P], src[:, 4 * q + t, 0:C + 1], idn)
                    ins.then_inc((b_tr, b_tr3)[k], 1)
                if n == 6:
                    pe.wait_ge(b_n2T, 2 * g + 2)
                    for t in range(T):
                        ins = te_.matmul(M1[:, t * C:(t + 1) * C], bT[:, t * P:(t + 1) * P], PW[:, :], start=True,
                                         stop=True)
                    ins.then_inc(b_pr, 1)
                if n == 11:
                    pe.wait_ge(late_in, 16 * 5)
                    pe.wait_ge(b_h3T, 2 * g + 2)
                    for t in range(T):
                        ins = te_.matmul(M1[:, t * E:(t + 1) * E], bT[:, t * P:(t + 1) * P], gw[:, :], start=True,
                                         stop=True)
                    ins.then_inc(b_gate, 1)
                if n == 13:
                    pe.wait_ge(b_oh, g + 1)
                    te_.matmul(M1[:, T * E:2 * T * E], tri[:, :], oh[:, :, 1:T + 1], start=True, stop=False,
                               skip_group_check=True)
                    te_.matmul(M1[:, T * E:2 * T * E], ones[:, :], before[:, :, 0:T], start=False, stop=True,
                               skip_group_check=True).then_inc(b_pos, 1)

            for n in range(17):
                front(0, n)
            pe.wait_ge(sel_done, 1)

            def step(s, has_front, has_back):
                pe.wait_ge(f_parts, s + 1)
                if has_back:
                    pe.wait_ge(s_scan, 16 * s)
                spread(Bp, 0, s, s_B)
                if has_back:
                    pe.wait_ge(s_ccp, 8 * s)
                spread(Cp, N, s, s_C)
                if has_back:
                    add_state(s - 1, 15)
                for n in range(16):
                    scan(s, n)
                    if has_back:
                        back(s - 1, n)
                    if has_front:
                        front(s + 1, n)
                if has_back:
                    back(s - 1, 16)

            step(0, True, False)
            with pe.Fori(1, B - 1) as s:
                step(s, True, True)
            step(B - 1, False, True)
            add_state(B - 1, 15)
            for n in range(17):
                back(B - 1, n)

            def turn(e):
                pe.wait_ge(e_in[e % 3], 16 * (e // 3 + 1))
                if e:
                    pe.wait_ge(e_xT, e)
                for k in range(ET):
                    ins = te_.transpose(Bp[0:C, k * P:(k + 1) * P], xe[:, e % 3, k, 0:C], idn)
                ins.then_inc(e_tr, 1)

            cols = [slice(0, HALF), slice(HALF, CAP)]
            turn(0)
            for e in range(E):
                pe.wait_ge(e_xT, e + 1)
                for k, dst in enumerate((Cp, Yp)):
                    if e:
                        pe.wait_ge((e_h0, e_h1)[k], e)
                    for c in cols:
                        ins = te_.matmul(dst[:, c], w1s[:, e, k * P:(k + 1) * P], xT[:, c], start=True, stop=True)
                    ins.then_inc(e_up, 1)
                if e + 1 < E:
                    turn(e + 1)
                pe.wait_ge(e_h0, e + 1)
                pe.wait_ge(e_h1, e + 1)
                if e >= 2:
                    pe.wait_ge(e_yo, e - 1)
                for k in range(ET):
                    for i, hid in enumerate((h0, h1)):
                        ins = te_.matmul((M0, M1)[e % 2][:, k * C:(k + 1) * C], hid[:, k * P:(k + 1) * P],
                                         w2s[:, e, i, :], start=(i == 0), stop=(i == 1))
                ins.then_inc(e_dn, 1)

        @block.vector
        def _(dve):
            ve = nc.vector
            X = mybir.AxisListType.X
            dve.wait_ge(w_in, 16 * 16)
            for k in range(TAPS):
                ins = ve.tensor_scalar(taps[:, k, :], wi[:, 0, :], cw[:, k:k + 1], None, ALU.mult)
            ins.then_inc(taps_done, 1)
            dve.wait_ge(pool_const, 4)
            ve.tensor_scalar(gfold[:, 0:C], ident[0:C, 0:C], gcol[:, :], None, ALU.mult)
            ve.tensor_copy(gfold[:, C:C + 1], bcol[:, :])
            ve.tensor_scalar(skipI[:, :], ident[0:C, 0:C], skcol[:, :], None, ALU.mult)

            def input_norm(k, b0, b1):
                c = slice(b0 * T, b1 * T)
                dve.wait_ge((x_first, x_rest)[k], 16)
                ve.reduce_sum(fs[:, 0, c], xs_in[:, b0:b1].rearrange("p b t c -> p (b t) c"), X).then_inc(n_sum, 1)
                dve.wait_ge(n_sq, k + 1)
                ve.reduce_sum(fs[:, 2, c], squares[:, c, :], X).then_inc(n_var, 1)

            def normed_tiles(f):
                dve.wait_ge(n_z, 1 if first(f) else 2)
                ve.tensor_copy(zt[:, :, 0:C], at_tiles(fz, f)).then_inc(f_z, 1)

            def front(f, n):
                if n in (2, 3):
                    q = n - 2
                    dve.wait_ge(f_top, 2 * f + q + 1)
                    ve.tensor_copy(xnT[C:P, 2 + q * HALF:2 + (q + 1) * HALF],
                                   xnT[0:C, 3 + q * HALF:3 + (q + 1) * HALF]).then_inc(f_bot, 1)
                if n == 12:
                    dve.wait_ge(f_hi, f + 1)
                    ve.tensor_tensor(rest[:, :, :], bc_psum, bc[:, :, 0, :], ALU.subtract).then_inc(f_rest, 1)
                    dve.wait_ge(f_rest, f + 1)
                    ve.tensor_copy(bc[:, :, 1, :], rest[:, :, :]).then_inc(f_mid, 1)
                    dve.wait_ge(f_mid, f + 1)
                    ve.tensor_tensor(bc[:, :, 2, :], rest[:, :, :], bc[:, :, 1, :], ALU.subtract).then_inc(f_lo, 1)
                if n == 13:
                    dve.wait_ge(f_exp, f + 1)
                    ve.tensor_scalar(big[:, :], te[:, :], 2.0 ** -10, None, ALU.is_ge).then_inc(f_big, 1)
                if n == 15:
                    dve.wait_ge(f_corr, f + 1)
                    dve.wait_ge(f_big, f + 1)
                    ve.tensor_tensor(te[:, :], te[:, :], at(du, f), ALU.subtract)
                    dve.drain()
                    ve.copy_predicated(te[:, :], big[:, :], tabs[:, :]).then_inc(f_log, 1)
                    dve.wait_ge(f_log, f + 1)
                    if not first(f):
                        dve.wait_ge(s_dA, 16 * f)
                    ve.tensor_tensor(delta[:, :], te[:, :], trel[:, :], ALU.add).then_inc(f_delta, 1)
                    dve.wait_ge(f_delta, f + 1)
                    ve.tensor_tensor(at(du, f), delta[:, :], at(u, f), ALU.mult).then_inc(f_du, 1)

            def scan(s, n):
                j, own = n // 2, n % 2 == 0
                dve.wait_ge(s_B, 16 * s + n + 1)
                ve.tensor_tensor(Bp[:, :], Bp[:, :], at(du, s), ALU.mult).then_inc(s_mul, 1)
                dve.wait_ge(s_mul, 16 * s + n + 1)
                dve.wait_ge(s_dA, 16 * s + n + 1)
                hb = h[:, 2 * (n % 2) + j % 2, :]
                if not own and not (first(s) and j < 2):
                    dve.wait_ge(s_pP, 8 * s + j - 1)
                ve.tensor_tensor_scan(hb, dA[:, n % 3, :], Bp[:, :], 0.0, ALU.mult, ALU.add).then_inc(s_scan, 1)
                if own:
                    dve.wait_ge(s_scan, 16 * s + n + 1)
                    dve.wait_ge(s_C, 16 * s + n + 1)
                    if not (first(s) and j < 2):
                        dve.wait_ge(s_sum, 16 * s + n - 3)
                    ve.tensor_tensor(prod[:, j % 2, :], Cp[:, :], hb, ALU.mult).then_inc(s_pD, 1)

            def back(g, n):
                if n == 0:
                    dve.wait_ge(s_sum, 16 * g + 16)
                    ve.scalar_tensor_tensor(yt[:, :], at(u, g), Dcol[:, :], Yp[:, :], ALU.mult,
                                            ALU.add).then_inc(b_yt, 1)
                if n == 1:
                    dve.wait_ge(b_yt, g + 1)
                    ve.tensor_tensor(yt[:, :], yt[:, :], at(sz, g), ALU.mult).then_inc(b_yg, 1)
                if n == 2:
                    dve.wait_ge(b_op, g + 1)
                    dve.wait_ge(f_skx, g + 1)
                    ve.tensor_tensor(y2[:, :, :], tiles(M1[:, :], C), at_tiles(skx, g), ALU.add).then_inc(b_y2, 1)
                    dve.wait_ge(b_y2, g + 1)
                    ve.reduce_sum(bs[:, 0, :], y2[:, :, :], X).then_inc(b_sum, 1)
                if n in (3, 8):
                    k = n // 8
                    dve.wait_ge((b_sq, b_sq3)[k], g + 1)
                    ve.reduce_sum(bs[:, 10 * k + 2, :], (n2, rows)[k][:, :, 0:C], X).then_inc((b_var, b_var3)[k], 1)
                if n == 7:
                    dve.wait_ge(b_pr, g + 1)
                    dve.wait_ge(b_sent, 16 + SENT * g)
                    t1 = rows[:, :, R_RES:R_RES + C]
                    ve.tensor_tensor(t1, tiles(M1[:, :], C), at_tiles(xs_in, g), ALU.add).then_inc(b_t1, 1)
                    dve.wait_ge(b_t1, g + 1)
                    ve.reduce_sum(bs[:, 10, :], t1, X).then_inc(b_sum3, 1)
                if n == 12:
                    link = Chain(dve, b_dve, g, 3)
                    lg = tiles(M1[:, 0:T * E], E)
                    dve.wait_ge(b_gate, g + 1)
                    link(ve.tensor_reduce(bs[:, 20, :], lg, X, ALU.max))
                    ve.tensor_tensor(ld[:, :, :], lg, over(bs[:, 20, :], E), ALU.subtract).then_inc(b_ld, 1)
                    dve.wait_ge(b_ld, g + 1)
                    link(ve.scalar_tensor_tensor(lrev[:, :, :], ld[:, :, :], 0.0, revc[:, :, :], ALU.is_equal,
                                                 ALU.mult))
                    link(ve.tensor_reduce(bs[:, 21, :], lrev[:, :, :], X, ALU.max))
                    link.end()
                    link = Chain(dve, b_dve2, g, 2)
                    link(ve.tensor_tensor(oh[:, :, 1:T + 1].rearrange("p e t -> p t e"), lrev[:, :, :],
                                          over(bs[:, 21, :], E), ALU.is_equal))
                    ve.tensor_tensor_scan(before[:, :, :].rearrange("p e t -> p (e t)"),
                                          resets[:, :, :].rearrange("p e t -> p (e t)"),
                                          oh[:, :, :].rearrange("p e t -> p (e t)"), 0.0, ALU.mult,
                                          ALU.add).then_inc(b_oh, 1)
                    dve.wait_ge(b_oh, g + 1)
                    link(ve.tensor_copy(oh[:, :, 0:1], before[:, :, T:T + 1]))
                    link.end()
                if n == 14:
                    dve.wait_ge(b_ex, g + 1)
                    link = Chain(dve, b_dve3, g, 7)
                    link(ve.reduce_sum(bs[:, 22, :], lex[:, :, :], X))
                    link(ve.reciprocal(rows[:, :, R_PRB:R_PRB + 1], bs[:, 22, :].unsqueeze(2)))
                    ve.tensor_copy(rows[:, :, R_ID:R_ID + 1].bitcast(I32), ids[:, bass.ds(g, 1), :].rearrange(
                        "p b t -> p t b"))
                    link(ve.tensor_scalar(bs[:, 23, :], bs[:, 21, :], -float(CAP), float(E * CAP), ALU.mult, ALU.add))
                    dve.wait_ge(b_pos, g + 1)
                    link(ve.tensor_tensor(lpo[:, :, :], M1[:, T * E:2 * T * E].rearrange("p (e t) -> p t e", e=E),
                                          oh[:, :, 1:T + 1].rearrange("p e t -> p t e"), ALU.mult))
                    link(ve.reduce_sum(bs[:, 24, :], lpo[:, :, :], X))
                    link(ve.tensor_scalar(bs[:, 25, :], bs[:, 24, :], float(CAP), float(2 * E * CAP), ALU.is_ge,
                                          ALU.mult))
                    link(ve.tensor_tensor(bs[:, 26, :], bs[:, 24, :], bs[:, 23, :], ALU.add))
                    link.end()
                    ve.tensor_tensor(chosen[:, :], bs[:, 26, :], bs[:, 25, :], ALU.add).then_inc(b_idx, 1)

            input_norm(0, 0, 1)
            ve.tensor_copy(identb[:, :], ident[:, :])
            dve.wait_ge(w_tr, 1)
            for dst, src in ((tapA[:, :], Bp[:, 0:128]), (tapB[:, :], Bp[:, 128:256]), (wzT[:, :], Bp[0:C, 256:384]),
                             (bcT[:, :], Bp[:, 384:416]), (dtwT[:, :], Bp[0:R, 512:640]), (woT[:, :], Bp[:, 640:704]),
                             (pwT[:, :], Bp[0:C, 704:768]), (b1c[:, :], Bp[:, 768:784])):
                ins = ve.tensor_copy(dst, src)
            ins.then_inc(w_ev, 1)
            dve.wait_ge(w_mm, 1)
            ve.tensor_copy(wdt[:, :], Cp[:, 0:P])
            ve.tensor_copy(PW[:, :], Cp[0:C + 1, HALF:HALF + C]).then_inc(w_ready, 1)
            dve.wait_ge(a_exp, 1)
            ve.tensor_scalar(aneg[:, :], aneg[:, :], -1.0, None, ALU.mult).then_inc(aneg_done, 1)
            normed_tiles(0)
            for n in range(4):
                front(0, n)
            input_norm(1, 1, B)
            ve.tensor_copy(sel[:, :, :], sel1[:, :].unsqueeze(2).broadcast_to([96, 2 * N, P])).then_inc(sel_done, 1)
            for n in range(4, 16):
                front(0, n)

            def step(s, has_front, has_back):
                if has_front:
                    normed_tiles(s + 1)
                dve.wait_ge(f_du, s + 1)
                for n in range(16):
                    scan(s, n)
                    if has_back:
                        back(s - 1, n)
                    if has_front:
                        front(s + 1, n)
                if has_back:
                    back(s - 1, 16)

            step(0, True, False)
            with dve.Fori(1, B - 1) as s:
                step(s, True, True)
            step(B - 1, False, True)
            for n in range(17):
                back(B - 1, n)

            dve.wait_ge(late_in, 16 * 5)
            for e in range(E):
                dve.wait_ge(e_up, 2 * e + 2)
                if e:
                    dve.wait_ge(e_dn, e)
                ve.tensor_scalar(h1[:, :], Yp[:, 0:CAP], b1c[:, 2 * e + 1:2 * e + 2], 0.0, ALU.add,
                                 ALU.max).then_inc(e_h1, 1)
                link = Chain(dve, e_dve, e, 6)
                y, cl, ok, diff = (ye[:, i] for i in range(4))
                dve.wait_ge(e_dn, e + 1)
                link(ve.tensor_tensor(y, tiles((M0, M1)[e % 2][:, 0:ET * C], C, ET),
                                      b2s[:, e, :].unsqueeze(1).broadcast_to([P, ET, C]), ALU.add))
                link(ve.tensor_tensor(y, y, xe[:, e % 3, :, R_PRB:R_PRB + 1].broadcast_to([P, ET, C]), ALU.mult))
                ve.tensor_tensor(diff, y, y, ALU.subtract).then_inc(e_diff, 1)
                ve.tensor_scalar(cl, y, 1e4, -1e4, ALU.min, ALU.max)
                link(ve.tensor_tensor(ok, y, y, ALU.is_equal))
                dve.wait_ge(e_diff, e + 1)
                ve.tensor_scalar(fin[:, :, :], diff, 0.0, None, ALU.is_equal)
                link(ve.tensor_tensor(cl, cl, ok, ALU.mult))
                link(ve.copy_predicated(cl, fin[:, :, :], y))
                if e >= 2:
                    dve.wait_ge(e_out[(e - 2) % 3], 16 * ET * ((e - 2) // 3 + 1))
                ve.tensor_tensor(yo[:, e % 2], cl, xe[:, e % 3, :, R_RES:R_RES + C], ALU.add).then_inc(e_yo, 1)
                link(ve.tensor_copy(ok[:, 0:1, 0:1], cl[:, 0:1, 0:1]))
                link.end()


_INS = ['x', 'L0_conv_ln_g', 'L0_conv_ln_b', 'L0_conv_in_proj_w', 'L0_conv_conv_w', 'L0_conv_conv_b',
        'L0_conv_x_proj_w', 'L0_conv_dt_proj_w', 'L0_conv_dt_proj_b', 'L0_conv_A_log', 'L0_conv_D',
        'L0_conv_out_proj_w', 'L0_conv_proj_w', 'L0_conv_proj_b', 'L0_conv_skip_scale', 'L0_ffn_gate_w',
        'L0_ffn_gate_b', 'L0_ffn_w1', 'L0_ffn_b1', 'L0_ffn_w2', 'L0_ffn_b2']
_OUTS = [((4, 32, 32, 64), 'float32')]


def kernel(**inputs):
    import numpy as _np
    import concourse.bacc as _bacc
    from concourse import mybir as _mybir
    from concourse.bass_utils import run_bass_kernel_spmd as _run

    nc = _bacc.Bacc("TRN2", target_bir_lowering=False, num_devices=1)
    arrays, args = {}, []
    for name in _INS:
        a = _np.ascontiguousarray(inputs[name])
        arrays[f"in_{name}_dram"] = a
        args.append(nc.dram_tensor(f"in_{name}_dram", a.shape, _mybir.dt.from_np(a.dtype), kind="ExternalInput").ap())
    for i, (shape, dtype) in enumerate(_OUTS):
        dt = _mybir.dt.from_np(_np.dtype(dtype))
        args.append(nc.dram_tensor(f"out_{i}_dram", shape, dt, kind="ExternalOutput").ap())
    metaformer_layer(nc, *args)
    r = _run(nc, [arrays], core_ids=[0])
    got = tuple(r.results[0][f"out_{i}_dram"] for i in range(len(_OUTS)))
    return got[0]
```

```python
from contextlib import ExitStack

import concourse.bass as bass
from concourse import mybir

ALU = mybir.AluOpType
ACT = mybir.ActivationFunctionType
AX = mybir.AxisListType.X
F32 = mybir.dt.float32
BF16 = mybir.dt.bfloat16
I32 = mybir.dt.int32

P = 128
B, H, W, C = 4, 32, 32, 64
L = H * W
T = L // P
DI = 2 * C
N = 16
R = 4
TAPS = 4
HALF = 512
E, F = 8, 256
CAP = (B * L * 5 // 4 + E - 1) // E
ET = CAP // P
LN_C_EPS, LN_EPS = 1e-6, 1e-5

R_ONE, R_RES, R_PRB, R_ID, ROW = C, C + 1, 2 * C + 1, 2 * C + 2, 2 * C + 3
NOWHERE = 1 << 20
SENT = 16 * T
BC_ALONE = 16


class Chain:

    def __init__(self, eng, sem, turn, steps):
        self.eng, self.sem, self.base, self.steps, self.n = eng, sem, turn * steps, steps, 0

    def __call__(self, ins):
        self.n += 1
        assert self.n <= self.steps
        ins.then_inc(self.sem, 1)
        self.eng.wait_ge(self.sem, self.base + self.n)

    def end(self):
        assert self.n == self.steps, (self.n, self.steps)


def metaformer_layer(nc, x, ln_g, ln_b, in_proj_w, conv_w, conv_b, x_proj_w, dt_proj_w, dt_proj_b, A_log,
                     D, out_proj_w, proj_w, proj_b, skip_scale, gate_w, gate_b, w1, b1, w2, b2, out):
    x_dram = x.rearrange("b h w c -> (b h w) c").rearrange("(b t p) c -> b p t c", b=B, p=P)
    out_rows = out.rearrange("b h w c -> (b h w) c")
    out_dram = out_rows.rearrange("(b t p) c -> b p t c", b=B, p=P)
    slots_dram = nc.dram_tensor("slots", (E * CAP, ROW), F32, kind="Internal").ap()

    with ExitStack() as ctx:
        def sb(name, shape, dt=F32):
            return ctx.enter_context(nc.sbuf_tensor(name, shape, dt))

        def sem(name):
            return ctx.enter_context(nc.semaphore(name))

        Bp = ctx.enter_context(nc.psum_tensor("Bp", [P, L], F32))
        Cp = ctx.enter_context(nc.psum_tensor("Cp", [P, L], F32))
        Yp = ctx.enter_context(nc.psum_tensor("Yp", [P, L], F32))
        M0 = ctx.enter_context(nc.psum_tensor("M0", [P, HALF], F32))
        M1 = ctx.enter_context(nc.psum_tensor("M1", [P, HALF], F32))

        ident = sb("ident", [P, P])
        sel1 = sb("sel1", [96, 2 * N], BF16)
        sel = sb("sel", [96, 2 * N, P], BF16)
        tri = sb("tri", [P, P], BF16)
        ones = sb("ones", [P, P], BF16)
        revc = sb("revc", [P, T, E])
        revi = sb("revi", [P, T, E], I32)
        ids = sb("ids", [P, B, T], I32)
        resets = sb("resets", [P, E, T + 1])
        mhalf = sb("mhalf", [P, B * T])
        invC = sb("invC", [P, B * T])
        zero = sb("zero", [P, T], I32)
        in_scale = sb("in_scale", [P, B * T])
        in_eps = sb("in_eps", [P, B * T])
        eps5 = sb("eps5", [P, T])
        gcol = sb("gcol", [C, 1])
        bcol = sb("bcol", [C, 1])
        cw = sb("cw", [P, TAPS])
        cb = sb("cb", [P, 1])
        xbc = sb("xbc", [2 * N, P])
        xdt = sb("xdt", [R, P])
        dtw = sb("dtw", [P, R])
        dtb = sb("dtb", [P, 1])
        alog = sb("alog", [P, N])
        aneg = sb("aneg", [P, N])
        Dcol = sb("Dcol", [P, 1])
        wo = sb("wo", [C, P])
        pw = sb("pw", [C, C])
        pb = sb("pb", [1, C])
        last1 = sb("last1", [1, C + 1])
        gfold = sb("gfold", [C, C + 1])
        skcol = sb("skcol", [P, 1])
        gskip = sb("gskip", [P, C])
        bskip = sb("bskip", [P, C])
        gw = sb("gw", [C + 1, E])
        w1s = sb("w1s", [P, E, F])
        w2s = sb("w2s", [P, E, 2, C])
        b1r = sb("b1r", [2 * E, P])
        b1c = sb("b1c", [P, 2 * E])
        b2s = sb("b2s", [P, E, C])
        tapA = sb("tapA", [P, P])
        tapB = sb("tapB", [P, P])
        wzT = sb("wzT", [C, P])
        bcT = sb("bcT", [P, 2 * N])
        identb = sb("identb", [P, P], BF16)
        dtwT = sb("dtwT", [R, P])
        woT = sb("woT", [P, C])
        pwT = sb("pwT", [C, C])
        wdt = sb("wdt", [P, P])
        PW = sb("PW", [C + 1, C])

        xs_in = sb("xs_in", [P, B, T, C])
        u = sb("u", [P, B, L])
        sz = sb("sz", [P, B, L])
        delta = sb("delta", [P, L])
        du = sb("du", [P, B, L])
        parts = sb("parts", [96, B, L], BF16)

        fs = sb("fs", [P, 6, B * T])
        fz = sb("fz", [P, B, T, C])
        skx = fz
        zt = sb("zt", [P, T, C + 1])
        xnT = sb("xnT", [P, L + 3])
        rest = sb("rest", [P, T, 2 * N])
        bc = sb("bc", [P, T, 3, 2 * N], BF16)
        small = sb("small", [P, L], mybir.dt.uint8)
        tabs = sb("tabs", [P, L])
        trel = sb("trel", [P, L])
        te = sb("te", [P, L])
        dA = sb("dA", [P, 3, L])
        bx = sb("bx", [P, 2, L])
        h = sb("h", [P, 3, L])
        prod = sb("prod", [P, 4, L])
        csb = sb("csb", [P, 2, L])
        yt = sb("yt", [P, L])
        yt_free = yt
        bs = sb("bs", [P, 28, T])
        y2 = sb("y2", [P, T, C])
        bxm = sb("bxm", [P, T, C])
        n2 = sb("n2", [P, T, C + 1])
        bT = sb("bT", [C + 1, L])
        rows = sb("rows", [P, T, ROW])
        ld = sb("ld", [P, T, E])
        lex = sb("lex", [P, T, E])
        lrev = sb("lrev", [P, T, E])
        lpo = sb("lpo", [P, T, E])
        oh = sb("oh", [P, E, T + 1], BF16)
        before = sb("before", [P, E, T + 1], BF16)
        chosen = sb("chosen", [P, T], I32)
        slot = sb("slot", [P, T], I32)
        fill = sb("fill", [P, ROW])
        def within(buf, start, *dims):
            size = 1
            for d in dims:
                size *= d
            flat = buf[:, :, :].rearrange("p a l -> p (a l)")[:, start:start + size]
            names = "abcd"[:len(dims)]
            if len(dims) == 1:
                return flat
            return flat.rearrange(f"p ({' '.join(names)}) -> p {' '.join(names)}",
                                  **{k: d for k, d in zip(names[1:], dims[1:])})

        wi = within(dA, 0, 2, C)
        taps = within(dA, L, TAPS, C)
        squares = within(prod, 0, B * T, C)
        rows4 = within(h, 0, 4, ET, ROW)
        rows3 = within(csb, 0, 3, ET, ROW)
        rows1 = within(bx, 0, 1, ET, ROW)
        xe = [rows4[:, i] for i in range(4)] + [rows3[:, i] for i in range(3)] + [rows1[:, 0]]
        xT = within(prod, 0, 2, CAP)
        h0 = within(prod, 2 * CAP, 2, CAP)
        h1 = within(prod, 4 * CAP, 2, CAP)
        ye = within(dA, 0, 4, ET, C)
        yo = within(dA, 4 * ET * C, 2, ET, C)
        fin = within(dA, 2 * L, ET, C).bitcast(I32)

        x_first, x_rest = sem("x_first"), sem("x_rest")
        w_first, w_in, late_in = sem("w_first"), sem("w_in"), sem("late_in")
        pool_const, pool_init = sem("pool_const"), sem("pool_init")
        sel_done, taps_done = sem("sel_done"), sem("taps_done")
        conv_tr, conv_ev, w_fold, w_tr, w_ev, w_mm, w_ready, aneg_done, a_exp = map(
            sem, "conv_tr conv_ev w_fold w_tr w_ev w_mm w_ready aneg_done a_exp".split())
        n_sum, n_mean, n_xm, n_sq, n_var, n_rstd, n_z = map(sem, "n_sum n_mean n_xm n_sq n_var n_rstd n_z".split())
        (f_z, f_tr, f_top, f_mx, f_xcr, f_mz, f_zr, f_silu, f_gate, f_skx, f_bc, f_hi, f_rest, f_mid, f_lo, f_btr,
         f_parts, f_dt, f_am, f_abs, f_exp, f_one, f_ln, f_sq, f_less, f_high, f_pick, f_delta, f_du) = map(sem, (
             "f_z f_tr f_top f_mx f_xcr f_mz f_zr f_silu f_gate f_skx f_bc f_hi f_rest f_mid f_lo f_btr "
             "f_parts f_dt f_am f_abs f_exp f_one f_ln f_sq f_less f_high f_pick f_delta f_du").split())
        s_B, s_mul, s_dA, s_scan, s_C, s_ccp, s_pD, s_pP, s_sum = map(sem, (
            "s_B s_mul s_dA s_scan s_C s_ccp s_pD s_pP s_sum").split())
        (b_yt, b_yg, b_op, b_y2, b_sum, b_xm, b_sq, b_var, b_n2, b_tr, b_n2T, b_pr, b_t1, b_sum3, b_sq3,
         b_var3, b_h3, b_tr3, b_h3T, b_gate, b_ld, b_ex, b_oh, b_pos, b_idx, b_pool, b_dve, b_dve2, b_dve3, b_res, b_sent, l_dve, l_var, l_rstd) = map(sem, (
             "b_yt b_yg b_op b_y2 b_sum b_xm b_sq b_var b_n2 b_tr b_n2T b_pr b_t1 b_sum3 b_sq3 "
             "b_var3 b_h3 b_tr3 b_h3T b_gate b_ld b_ex b_oh b_pos b_idx b_pool b_dve b_dve2 b_dve3 b_res b_sent l_dve l_var l_rstd").split())
        fill_done = sem("fill_done")
        e_in = [sem(f"e_in{e}") for e in range(E)]
        e_out = [sem(f"e_out{i}") for i in range(2)]
        e_zero, e_tr, e_xT, e_up, e_h0, e_h1, e_dn, e_y, e_yo, e_dve, e_diff = map(sem, (
            "e_zero e_tr e_xT e_up e_h0 e_h1 e_dn e_y e_yo e_dve e_diff").split())

        def at(buf, b):
            return buf[:, bass.ds(b, 1), :].rearrange("p b l -> p (b l)")

        def at_half(buf, b, q):
            return buf[:, bass.ds(b, 1), q * HALF:(q + 1) * HALF].rearrange("p b l -> p (b l)")

        def at_tiles(buf, b):
            return buf[:, bass.ds(b, 1), :, :].rearrange("p b t c -> p (b t) c")

        def over(col, n):
            return col.unsqueeze(2).broadcast_to([P, col.shape[1], n])

        def first(b):
            return isinstance(b, int) and b == 0

        def last(g):
            return isinstance(g, int) and g == B - 1

        def back_bank(g, stage, q=0):
            if last(g):
                return {"turn": (M1[:, :], M0[:, :])[q], "proj": Bp[:, 0:HALF], "gate": Cp[:, 0:HALF]}[stage]
            return M1[:, :]

        def tiles(psum, n, k=T):
            return psum.rearrange("p (t c) -> p t c", t=k)[:, :, 0:n]

        HB = [slice(0, HALF), slice(HALF, L)]

        def bank(f, stage, q):
            if stage == "rows" or stage == "norm":
                return {"norm": (M0, M1), "rows": (M1,)}[stage][q][:, :]
            if not first(f):
                return (M1 if (stage, q) == ("conv", 0) else M0)[:, :]
            return {"conv": Yp, "gate": Cp, "step": Yp}[stage][:, HB[q]]

        def rows_psum(f):
            return bank(f, "rows", 0)[:, 0:T * 2 * N].rearrange("p (t r) -> p t r", t=T)

        block = ctx.enter_context(nc.Block())
        M0b = M0[:, :].bitcast(BF16)

        @block.sync
        def _(sp):
            sp.dma_start(xs_in[:, 0], x_dram[0]).then_inc(x_first, 16)
            for dst, src in ((wi[:, :, :], in_proj_w.rearrange("(h p) c -> p h c", p=P)), (cw[:, :], conv_w),
                             (gcol[:, :], ln_g.unsqueeze(1)), (bcol[:, :], ln_b.unsqueeze(1)),
                             (cb[:, :], conv_b.unsqueeze(1))):
                sp.dma_start(dst, src).then_inc(w_first, 16)
            for dst, src in ((dtb[:, :], dt_proj_b.unsqueeze(1)),
                             (xbc[:, :], x_proj_w[R:R + 2 * N, :]), (xdt[:, :], x_proj_w[0:R, :]),
                             (dtw[:, :], dt_proj_w), (alog[:, :], A_log), (Dcol[:, :], D.unsqueeze(1)),
                             (wo[:, :], out_proj_w), (pw[:, :], proj_w), (pb[:, :], proj_b.unsqueeze(0)),
                             (skcol[:, :], skip_scale.unsqueeze(0).broadcast_to([P, 1])),
                             (gskip[:, :], ln_g.unsqueeze(0).broadcast_to([P, C])),
                             (bskip[:, :], ln_b.unsqueeze(0).broadcast_to([P, C])),
                             (b1r[:, :], b1.rearrange("e (h f) -> (e h) f", h=2))):
                sp.dma_start(dst, src).then_inc(w_in, 16)
            sp.dma_start(xs_in[:, 1:B], x_dram[1:B].rearrange("b p t c -> p b t c")).then_inc(x_rest, 16)
            for dst, src in ((gw[0:C, :], gate_w), (gw[C:C + 1, :], gate_b.unsqueeze(0)),
                             (w1s[0:C, :, :], w1.rearrange("e c f -> c e f")),
                             (w2s[:, :, :, :], w2.rearrange("e (h f) c -> f e h c", h=2)),
                             (b2s[:, :, :], b2.unsqueeze(0).broadcast_to([P, E, C]))):
                sp.dma_start(dst, src).then_inc(late_in, 16)
            sp.wait_ge(b_sent, 16 + SENT * B)
            for e in range(E):
                sp.dma_start(xe[e], slots_dram[e * CAP:(e + 1) * CAP, :].rearrange("(k p) r -> p k r", p=P)
                             ).then_inc(e_in[e], 16)

        @block.gpsimd
        def _(pool):
            po = nc.gpsimd
            po.memset(ident[:, :], 0.0).then_inc(pool_init, 1)
            po.memset(sel1[:, :], 0.0).then_inc(pool_init, 1)
            po.memset(tri[:, :], 1.0).then_inc(pool_init, 1)
            po.memset(ones[:, :], 1.0)
            po.memset(mhalf[:, :], -0.5)
            po.memset(invC[:, :], 1.0 / C)
            po.memset(zero[:, :], 0)
            po.memset(in_scale[:, :], (1.0 + LN_EPS) / C)
            po.memset(in_eps[:, :], LN_C_EPS * LN_EPS)
            po.memset(eps5[:, :], LN_EPS)
            po.memset(resets[:, :, :], 1.0)
            po.memset(last1[:, :], 0.0)
            po.memset(n2[:, :, C:C + 1], 1.0)
            po.memset(zt[:, :, C:C + 1], 1.0)
            po.memset(rows[:, :, R_ONE:R_ONE + 1], 1.0)
            po.memset(xnT[:, 0:3], 0.0)
            po.memset(oh[:, :, 0:1], 0.0)
            po.memset(fill[:, :], 0.0).then_inc(fill_done, 1)
            po.iota(revi[:, :, :], pattern=[[0, T], [-1, E]], base=E, channel_multiplier=0)
            po.iota(ids[:, :, :], pattern=[[L, B], [P, T]], base=0, channel_multiplier=1).then_inc(pool_init, 1)
            pool.wait_ge(pool_init, 4)
            pool.wait_ge(fill_done, 1)
            po.affine_select(out=ident[:, :], in_=ident[:, :], compare_op=ALU.not_equal, fill=1.0, base=0,
                             pattern=[[-1, P]], channel_multiplier=1)
            po.iota(fill[:, R_ID:R_ID + 1].bitcast(I32), pattern=[[0, 1]], base=NOWHERE,
                    channel_multiplier=0).then_inc(fill_done, 1)
            po.affine_select(out=tri[:, :], in_=tri[:, :], compare_op=ALU.is_gt, fill=0.0, base=0,
                             pattern=[[1, P]], channel_multiplier=-1)
            po.memset(resets[:, :, 0:1], 0.0)
            po.memset(last1[:, C:C + 1], 1.0)
            for k in range(3):
                po.affine_select(out=sel1[:, :], in_=sel1[:, :], compare_op=ALU.not_equal, fill=1.0, base=-32 * k,
                                 pattern=[[-1, 2 * N]], channel_multiplier=1).then_inc(pool_const, 1)
                pool.wait_ge(pool_const, k + 1)
            po.tensor_copy(revc[:, :, :], revi[:, :, :]).then_inc(pool_const, 1)
            pool.wait_ge(pool_const, 4)
            pool.wait_ge(fill_done, 2)
            po.dma_start(slots_dram.rearrange("(k p) r -> p k r", p=P),
                         fill[:, :].unsqueeze(1).broadcast_to([P, E * ET, ROW])).then_inc(b_sent, 16)

            def rstd(link, s, var_sum, o):
                link(po.tensor_tensor(s[:, o, :], s[:, var_sum, :], invC[:, 0:T], ALU.mult))
                link(po.tensor_tensor(s[:, o + 1, :], s[:, o, :], eps5[:, :], ALU.add))
                link(po.tensor_tensor(s[:, o + 2, :], s[:, o + 1, :], mhalf[:, 0:T], ALU.pow))

            def input_norm(k, b0, b1):
                c, m = slice(b0 * T, b1 * T), (b1 - b0) * T
                z, xin = (buf[:, b0:b1].rearrange("p b t c -> p (b t) c") for buf in (fz, xs_in))
                pool.wait_ge(n_sum, k + 1)
                po.tensor_tensor(fs[:, 1, c], fs[:, 0, c], invC[:, 0:m], ALU.mult).then_inc(n_mean, 1)
                pool.wait_ge(n_mean, k + 1)
                po.tensor_tensor(z, xin, over(fs[:, 1, c], C), ALU.subtract).then_inc(n_xm, 1)
                pool.wait_ge(n_var, k + 1)
                link = Chain(pool, n_rstd, k, 3)
                link(po.tensor_tensor(fs[:, 3, c], fs[:, 2, c], in_scale[:, 0:m], ALU.mult))
                link(po.tensor_tensor(fs[:, 4, c], fs[:, 3, c], in_eps[:, 0:m], ALU.add))
                link(po.tensor_tensor(fs[:, 5, c], fs[:, 4, c], mhalf[:, 0:m], ALU.pow))
                link.end()
                po.tensor_tensor(z, z, over(fs[:, 5, c], C), ALU.mult).then_inc(n_z, 1)

            def scan(s, n):
                j = n // 2
                pool.wait_ge(s_ccp, 8 * s + j + 1)
                pool.wait_ge(s_scan, 16 * s + n + 1)
                if not (first(s) and j < 2):
                    pool.wait_ge(s_sum, 16 * s + n - 3)
                po.tensor_tensor(prod[:, 2 + j % 2, :], h[:, 1 + j % 2, :], csb[:, j % 2, :],
                                 ALU.mult).then_inc(s_pP, 1)

            def front(f, n):
                if n == 2:
                    if first(f):
                        pool.wait_ge(f_z, 1)
                        pool.wait_ge(w_fold, 1)
                    po.tensor_tensor(at_tiles(fz, f), at_tiles(fz, f), gskip[:, :].unsqueeze(1).broadcast_to([P, T, C]),
                                     ALU.mult)
                    pool.drain()
                    po.tensor_tensor(at_tiles(skx, f), at_tiles(fz, f), bskip[:, :].unsqueeze(1).broadcast_to([P, T, C]),
                                     ALU.add).then_inc(f_skx, 1)
                if n == 13:
                    pool.wait_ge(f_ln, f + 1)
                    po.tensor_tensor(tabs[:, :], yt_free[:, :], tabs[:, :], ALU.subtract).then_inc(f_less, 1)
                    po.tensor_tensor(trel[:, :], trel[:, :], at(du, f), ALU.add).then_inc(f_high, 1)

            def back(g, n):
                if last(g) and n in (4, 9):
                    k = n // 9
                    pool.wait_ge(l_var, k + 1)
                    po.tensor_tensor(bs[:, 10 * k + 5, :], bs[:, 10 * k + 4, :], mhalf[:, 0:T],
                                     ALU.pow).then_inc(l_rstd, 1)
                if not last(g) and n in (3, 8):
                    k = 0 if n == 3 else 1
                    pool.wait_ge((b_sum, b_sum3)[k], g + 1)
                    o = 10 * k
                    link = Chain(pool, b_pool, 2 * g + k, 4)
                    link(po.tensor_tensor(bs[:, o + 1, :], bs[:, o, :], invC[:, 0:T], ALU.mult))
                    src = (y2[:, :, :], rows[:, :, R_RES:R_RES + C])[k]
                    po.tensor_tensor(bxm[:, :, :], src, over(bs[:, o + 1, :], C), ALU.subtract).then_inc(b_xm, 1)
                    pool.wait_ge(b_xm, 2 * g + k + 1)
                    po.tensor_tensor((n2, rows)[k][:, :, 0:C], bxm[:, :, :], bxm[:, :, :],
                                     ALU.mult).then_inc((b_sq, b_sq3)[k], 1)
                    links[k] = link
                if not last(g) and n in (4, 9):
                    k = 0 if n == 4 else 1
                    o = 10 * k
                    pool.wait_ge((b_var, b_var3)[k], g + 1)
                    link = links[k]
                    rstd(link, bs, o + 2, o + 3)
                    link.end()
                    dst = (n2[:, :, 0:C], rows[:, :, 0:C])[k]
                    po.tensor_tensor(dst, bxm[:, :, :], over(bs[:, o + 5, :], C),
                                     ALU.mult).then_inc((b_n2, b_h3)[k], 1)
                if n == 16:
                    pool.wait_ge(b_idx, g + 1)
                    po.tensor_tensor(slot[:, :], chosen[:, :], zero[:, :], ALU.add)
                    pool.drain()
                    for t in range(T):
                        po.indirect_dma_start(slots_dram[:, :], bass.IndirectOffsetOnAxis(ap=slot[:, t:t + 1], axis=0),
                                              rows[:, t, :], None, bounds_check=last_slot,
                                              oob_is_err=False).then_inc(b_sent, 16)
                    po.dma_start(out_dram[bass.ds(g, 1)].rearrange("b p t c -> p (b t) c"),
                                 rows[:, :, R_RES:R_RES + C]).then_inc(b_res, 16)

            links = [None, None]
            last_slot = po.to_reg(E * CAP - 1)
            input_norm(0, 0, 1)
            input_norm(1, 1, B)

            front(0, 2)

            def step(s, has_front, has_back):
                for n in range(16):
                    if has_back:
                        back(s - 1, n)
                    if has_front:
                        front(s + 1, n)
                    if n % 2:
                        scan(s, n)
                if has_back:
                    back(s - 1, 16)

            step(0, True, False)
            with pool.Fori(1, B - 1) as s:
                step(s, True, True)
            step(B - 1, False, True)
            for n in range(17):
                back(B - 1, n)
            pool.wait_ge(b_res, 16 * B)
            for e in range(E):
                pool.wait_ge(e_yo, e + 1)
                for k in range(ET):
                    po.indirect_dma_start(out_rows, bass.IndirectOffsetOnAxis(
                        ap=xe[e][:, k, R_ID:R_ID + 1].bitcast(I32), axis=0), yo[:, e % 2, k, :], None,
                        bounds_check=B * L - 1, oob_is_err=False).then_inc(e_out[e % 2], 16)
            for i in range(2):
                pool.wait_ge(e_out[i], 16 * ET * len(range(i, E, 2)))

        @block.scalar
        def _(act):
            ac = nc.scalar

            def act_set():
                ac.preload_act_table_set("natural_log_exp_and_others")

            def front(f, n):
                if n == 0:
                    if first(f):
                        act.wait_ge(w_first, 16 * 5)
                    for q in range(2):
                        act.wait_ge(f_tr, 2 * f + q + 1)
                        ac.activation(xnT[0:C, 3 + q * HALF:3 + (q + 1) * HALF], bank(f, "norm", q)[0:C], ACT.Identity,
                                      bias=bcol[:, :], scale=gcol[:, :])
                        ac.activation(xnT[C:P, 2 + q * HALF:2 + (q + 1) * HALF], bank(f, "norm", q)[0:C],
                                      ACT.Identity, bias=bcol[:, :], scale=gcol[:, :]).then_inc(f_top, 1)
                if first(f):
                    if n in (3, 4):
                        q = n - 3
                        act.wait_ge(f_mx, q + 1)
                        ac.activation(u[:, 0, HB[q]], bank(f, "conv", q), ACT.Silu, bias=cb[:, :])
                        ins = ac.activation(yt_free[:, HB[q]], bank(f, "conv", q), ACT.Silu, bias=cb[:, :])
                        if q == 1:
                            ins.then_inc(f_silu, 1)
                    if n in (5, 6):
                        q = n - 5
                        act.wait_ge(f_mz, q + 1)
                        ins = ac.activation(sz[:, 0, HB[q]], bank(f, "gate", q), ACT.Silu)
                        if q == 1:
                            ins.then_inc(f_gate, 1)
                    if n == 7:
                        act_set()
                else:
                    if n in (3, 4):
                        q = n - 3
                        act.wait_ge(f_mx, 2 * f + q + 1)
                        ac.activation(at_half(u, f, q), bank(f, "conv", q), ACT.Identity, bias=cb[:, :]).then_inc(f_xcr, 1)
                    if n in (5, 6):
                        q = n - 5
                        act.wait_ge(f_mz, 2 * f + q + 1)
                        ac.activation(at_half(sz, f, q), M0[:, :], ACT.Copy).then_inc(f_zr, 1)
                    if n == 7:
                        act.drain()
                        ac.activation(yt_free[:, :], at(u, f), ACT.Silu)
                        ac.activation(at(u, f), at(u, f), ACT.Silu).then_inc(f_silu, 1)
                        ac.activation(at(sz, f), at(sz, f), ACT.Silu).then_inc(f_gate, 1)
                        act_set()
                if n == (BC_ALONE if first(f) else 9):
                    act.wait_ge(f_bc, f + 1)
                    ac.activation(bc[:, :, 0, :], rows_psum(f), ACT.Copy).then_inc(f_hi, 1)
                if first(f) and n in (10, 11):
                    act.wait_ge(f_dt, n - 9)
                    ac.activation(tabs[:, HB[n - 10]], bank(f, "step", n - 10), ACT.Abs,
                                  bias=dtb[:, :]).then_inc(f_abs, 1)
                if first(f) and n == 11:
                    act.drain()
                    ac.activation(at(du, f), tabs[:, :], ACT.Exp, scale=-1.0).then_inc(f_exp, 1)
                if first(f) and n == 12:
                    act.wait_ge(f_one, 1)
                    ac.activation(tabs[:, :], bx[:, 0, :], ACT.Ln).then_inc(f_ln, 1)
                    ac.activation(te[:, :], at(du, f), ACT.Square, scale=0.5 ** 0.5).then_inc(f_sq, 1)
                if not first(f) and n in (10, 11):
                    q = n - 10
                    act.wait_ge(f_dt, 2 * f + q + 1)
                    ac.activation(tabs[:, HB[q]], bank(f, "step", q), ACT.Abs, bias=dtb[:, :])
                    ac.activation(trel[:, HB[q]], bank(f, "step", q), ACT.Relu, bias=dtb[:, :]).then_inc(f_am, 1)
                if not first(f) and n == 11:
                    act.drain()
                    ac.activation(at(du, f), tabs[:, :], ACT.Exp, scale=-1.0)
                    act.drain()
                    ac.activation(yt_free[:, :], at(du, f), ACT.Copy, bias=1.0)
                if not first(f) and n == 12:
                    act.drain()
                    ac.activation(tabs[:, :], yt_free[:, :], ACT.Ln)
                    ac.activation(yt_free[:, :], yt_free[:, :], ACT.Copy, bias=-1.0).then_inc(f_ln, 1)
                    ac.activation(te[:, :], at(du, f), ACT.Square, scale=0.5 ** 0.5).then_inc(f_sq, 1)
                if n == 13:
                    act.wait_ge(f_btr, f + 1)
                    ac.activation(at(parts, f), M0b[0:96, :], ACT.Copy).then_inc(f_parts, 1)

            def decay(s, n):
                if n >= 3:
                    act.wait_ge(s_scan, 16 * s + n - 2)
                elif not first(s):
                    act.wait_ge(s_scan, 16 * s - (15 - n) % 3)
                ac.activation(dA[:, n % 3, :], delta[:, :], ACT.Exp, scale=aneg[:, n:n + 1]).then_inc(s_dA, 1)

            def scan(s, n):
                if n + 2 < 16:
                    decay(s, n + 2)
                if n % 2:
                    j = n // 2
                    act.wait_ge(s_C, 16 * s + n + 1)
                    if not (first(s) and j < 2):
                        act.wait_ge(s_pP, 8 * s + j - 1)
                    ac.activation(csb[:, j % 2, :], Cp[:, :], ACT.Copy).then_inc(s_ccp, 1)

            def back(g, n):
                if n in (5, 6, 10, 11):
                    k, q = n // 10, (n - 5) % 5
                    act.wait_ge((b_tr, b_tr3)[k], 2 * g + q + 1)
                    ac.activation(bT[:, HB[q]], back_bank(g, "turn", q)[0:C + 1], ACT.Copy).then_inc((b_n2T, b_h3T)[k], 1)
                if n == 14:
                    act.wait_ge(b_ld, g + 1)
                    ac.activation(lex[:, :, :], ld[:, :, :], ACT.Exp).then_inc(b_ex, 1)

            ac.preload_act_table(ACT.Silu)

            def input_norm(k, b0, b1):
                act.wait_ge(n_xm, k + 1)
                ac.activation(squares[:, b0 * T:b1 * T, :], fz[:, b0:b1].rearrange("p b t c -> p (b t) c"),
                              ACT.Square).then_inc(n_sq, 1)

            input_norm(0, 0, 1)
            for n in range(8):
                front(0, n)
            act.wait_ge(w_in, 16 * 13)
            ac.activation(aneg[:, :], alog[:, :], ACT.Exp).then_inc(a_exp, 1)
            input_norm(1, 1, B)
            for n in (10, 11, BC_ALONE, 12, 13):
                front(0, n)
            act.wait_ge(aneg_done, 1)

            def step(s, has_front, has_back):
                act.wait_ge(f_delta, s + 1)
                decay(s, 0)
                decay(s, 1)
                for n in range(16):
                    scan(s, n)
                    if has_back and n < 10:
                        back(s - 1, n)
                    if has_front:
                        front(s + 1, n)
                    if has_back and n >= 10:
                        back(s - 1, n)

            step(0, True, False)
            with act.Fori(1, B - 1) as s:
                step(s, True, True)
            step(B - 1, False, True)
            for n in range(17):
                back(B - 1, n)
            def channels(e):
                act.wait_ge(e_tr, e + 1)
                if e >= 2:
                    act.wait_ge(e_up, 2 * (e - 1))
                ac.activation(xT[0:C, e % 2, :], Bp[0:C, 0:CAP], ACT.Copy).then_inc(e_xT, 1)

            channels(0)
            for e in range(E):
                act.wait_ge(e_up, 2 * e + 1)
                if e >= 2:
                    act.wait_ge(e_dn, e - 1)
                ac.activation(h0[:, e % 2, :], Cp[:, 0:CAP], ACT.Relu, bias=b1c[:, 2 * e:2 * e + 1]).then_inc(e_h0, 1)
                act.wait_ge(e_up, 2 * e + 2)
                ac.activation(h1[:, e % 2, :], Yp[:, 0:CAP], ACT.Relu,
                              bias=b1c[:, 2 * e + 1:2 * e + 2]).then_inc(e_h1, 1)
                if e + 1 < E:
                    channels(e + 1)

        @block.tensor
        def _(pe):
            te_ = nc.tensor
            idn = ident[:, :]
            def conv_weights():
                pe.wait_ge(w_first, 16 * 5)
                pe.wait_ge(pool_const, 4)
                te_.transpose(Cp[0:C, 256:384], wi[:, 1, :], idn)
                pe.wait_ge(taps_done, 1)
                te_.transpose(Cp[:, 0:128], taps[:, 0:2, :].rearrange("p k c -> p (k c)"), idn)
                te_.transpose(Cp[:, 128:256], taps[:, 2:4, :].rearrange("p k c -> p (k c)"), idn).then_inc(conv_tr, 1)

            def other_weights():
                te_.transpose(Bp[:, 384:416], xbc[:, :], ident[0:2 * N, 0:2 * N])
                te_.transpose(Bp[0:R, 512:640], dtw[:, :], idn)
                te_.transpose(Bp[:, 640:704], wo[:, :], ident[0:C, 0:C])
                te_.transpose(Bp[0:C, 704:768], pw[:, :], ident[0:C, 0:C])
                te_.transpose(Bp[:, 768:784], b1r[:, :], ident[0:2 * E, 0:2 * E]).then_inc(w_tr, 1)

            def weight_products():
                pe.wait_ge(w_ev, 1)
                te_.matmul(Bp[:, 0:P], xdt[:, :], dtwT[:, :], start=True, stop=True)
                te_.matmul(Bp[0:C + 1, 784:784 + C], gfold[:, :], pwT[:, :], start=True, stop=False)
                te_.matmul(Bp[0:C + 1, 784:784 + C], last1[:, :], pb[:, :], start=False, stop=True).then_inc(w_mm, 1)
                pe.wait_ge(w_ready, 1)

            def front(f, n):
                if n == 0:
                    pe.wait_ge(f_z, f + 1)
                    if not first(f):
                        pe.wait_ge(f_parts, f)
                    for q in range(2):
                        for t in range(4):
                            ins = te_.transpose(bank(f, "norm", q)[0:C + 1, t * P:(t + 1) * P], zt[:, 4 * q + t, :],
                                                idn)
                        ins.then_inc(f_tr, 1)
                if n in (2, 3):
                    q = n - 2
                    pe.wait_ge(f_top, 2 * f + q + 1)
                    if q == 1 and not (isinstance(f, int) and f <= 1):
                        pe.wait_ge(b_y2, f - 1)
                    if first(f):
                        pe.wait_ge(conv_ev, 1)
                    dst = bank(f, "conv", q)
                    te_.matmul(dst, tapA[:, :], xnT[:, q * HALF:(q + 1) * HALF], start=True, stop=False)
                    te_.matmul(dst, tapB[:, :], xnT[:, 2 + q * HALF:2 + (q + 1) * HALF], start=False,
                               stop=True).then_inc(f_mx, 1)
                if n in (4, 5):
                    q = n - 4
                    if not first(f):
                        pe.wait_ge((f_xcr, f_zr)[q], 2 * f - q)
                    te_.matmul(bank(f, "gate", q), wzT[:, :], xnT[0:C, 3 + q * HALF:3 + (q + 1) * HALF], start=True,
                               stop=True).then_inc(f_mz, 1)
                if n in (9, 10):
                    q = n - 9
                    if first(f):
                        pe.wait_ge(f_silu, f + 1)
                    else:
                        if q == 0:
                            pe.wait_ge(f_zr, 2 * f)
                        else:
                            pe.wait_ge(f_am, 2 * f - 1)
                    te_.matmul(bank(f, "step", q), wdt[:, :], at_half(u, f, q), start=True, stop=True).then_inc(f_dt, 1)
                if n == 8:
                    pe.wait_ge(f_silu, f + 1)
                    if not (isinstance(f, int) and f <= 1):
                        pe.wait_ge(b_t1, f - 1)
                    for t in range(T):
                        ins = te_.matmul(bank(f, "rows", 0)[:, t * 2 * N:(t + 1) * 2 * N], yt_free[:, t * P:(t + 1) * P], bcT[:, :],
                                         start=True, stop=True)
                    ins.then_inc(f_bc, 1)
                if n == 12:
                    pe.wait_ge(f_lo, f + 1)
                    if not first(f):
                        pe.wait_ge(f_am, 2 * f)
                    for t in range(T):
                        ins = te_.transpose(M0b[0:96, t * P:(t + 1) * P],
                                            bc[:, t, :, :].rearrange("p k r -> p (k r)"), identb[:, :])
                    ins.then_inc(f_btr, 1)

            def spread(dst, row, s, done):
                for q in range(2):
                    ins = te_.matmul(dst[:, HB[q]], sel[:, row, :], at_half(parts, s, q), start=True, stop=True)
                ins.then_inc(done, 1)

            def add_state(s, n):
                j = n // 2
                pe.wait_ge((s_pD, s_pP)[n % 2], 8 * s + j + 1)
                if n == 0 and not first(s):
                    pe.wait_ge(b_yt, s)
                for q in range(2):
                    ins = te_.matmul(Yp[:, HB[q]], idn, prod[:, 2 * (n % 2) + j % 2, HB[q]], start=(n == 0),
                                     stop=(n == 15), skip_group_check=True)
                ins.then_inc(s_sum, 1)

            def spread_B(s, n):
                pe.wait_ge(s_mul, 16 * s + n)
                spread(Bp, n, s, s_B)

            def spreads(s, n):
                if n + 2 < 16:
                    spread_B(s, n + 2)
                if n + 1 < 16:
                    pe.wait_ge((s_pD, s_ccp)[n % 2], 8 * s + n // 2 + 1)
                    spread(Cp, N + n + 1, s, s_C)

            def back(g, n):
                if n == 1:
                    pe.wait_ge(b_yg, g + 1)
                    for t in range(T):
                        ins = te_.matmul(M0[:, t * C:(t + 1) * C], yt[:, t * P:(t + 1) * P], woT[:, :], start=True,
                                         stop=True)
                    ins.then_inc(b_op, 1)
                if n in (4, 5, 10, 11):
                    k, q = n // 10, (n - 4) % 6
                    if q == 0:
                        pe.wait_ge((b_n2, b_h3)[k], g + 1)
                        pe.wait_ge((b_y2, b_t1)[k], g + 1)
                    else:
                        if not last(g):
                            pe.wait_ge((b_n2T, b_h3T)[k], 2 * g + 1)
                    src = (n2, rows)[k]
                    for t in range(4):
                        ins = te_.transpose(back_bank(g, "turn", q)[0:C + 1, t * P:(t + 1) * P], src[:, 4 * q + t, 0:C + 1], idn)
                    ins.then_inc((b_tr, b_tr3)[k], 1)
                if n == 6:
                    for t in range(T):
                        if t == 0 and last(g):
                            pe.wait_ge(b_n2T, 2 * g + 1)
                        if t == (T // 2 if last(g) else 0):
                            pe.wait_ge(b_n2T, 2 * g + 2)
                        ins = te_.matmul(back_bank(g, "proj")[:, t * C:(t + 1) * C], bT[:, t * P:(t + 1) * P], PW[:, :], start=True,
                                         stop=True)
                    ins.then_inc(b_pr, 1)
                if n == 12:
                    pe.wait_ge(late_in, 16 * 5)
                    for t in range(T):
                        if t == 0 and last(g):
                            pe.wait_ge(b_h3T, 2 * g + 1)
                        if t == (T // 2 if last(g) else 0):
                            pe.wait_ge(b_h3T, 2 * g + 2)
                        ins = te_.matmul(back_bank(g, "gate")[:, t * E:(t + 1) * E], bT[:, t * P:(t + 1) * P], gw[:, :], start=True,
                                         stop=True)
                    ins.then_inc(b_gate, 1)
                if n == 14:
                    pe.wait_ge(b_oh, g + 1)
                    te_.matmul(M1[:, T * E:2 * T * E], tri[:, :], oh[:, :, 1:T + 1], start=True, stop=False,
                               skip_group_check=True)
                    te_.matmul(M1[:, T * E:2 * T * E], ones[:, :], before[:, :, 0:T], start=False, stop=True,
                               skip_group_check=True).then_inc(b_pos, 1)

            conv_weights()
            for n in range(7):
                front(0, n)
            pe.wait_ge(w_fold, 1)
            other_weights()
            weight_products()
            for n in (9, 10, 8, 12):
                front(0, n)
            pe.wait_ge(sel_done, 1)

            sums = [[], [0], []] + [[n - 2] for n in range(3, 16)]

            def step(s, has_front, has_back):
                pe.wait_ge(f_parts, s + 1)
                if has_back:
                    pe.wait_ge(s_mul, 16 * s)
                spread(Bp, 0, s, s_B)
                if has_back:
                    pe.wait_ge(s_ccp, 8 * s)
                spread(Cp, N, s, s_C)
                if has_back:
                    add_state(s - 1, 14)
                spread_B(s, 1)
                if has_back:
                    add_state(s - 1, 15)
                for n in range(16):
                    for m in sums[n]:
                        add_state(s, m)
                    if n in (4, 6):
                        spreads(s, n)
                    if has_front:
                        front(s + 1, n)
                    if has_front and n == 1:
                        pe.wait_ge(f_top, 2 * s + 3)
                    if has_front and n == 4:
                        pe.wait_ge(f_xcr, 2 * s + 1)
                    if has_front and n == 10:
                        pe.wait_ge(f_rest, s + 2)
                    if has_back:
                        back(s - 1, n)
                    if n not in (4, 6):
                        spreads(s, n)
                if has_back:
                    back(s - 1, 16)

            step(0, True, False)
            with pe.Fori(1, B - 1) as s:
                step(s, True, True)
            step(B - 1, False, True)
            for n in range(14, 16):
                add_state(B - 1, n)
            for n in range(17):
                back(B - 1, n)

            def turn(e):
                pe.wait_ge(e_in[e], 16)
                if e:
                    pe.wait_ge(e_xT, e)
                for k in range(ET):
                    ins = te_.transpose(Bp[0:C, k * P:(k + 1) * P], xe[e][:, k, 0:C], idn)
                ins.then_inc(e_tr, 1)

            def up(e):
                pe.wait_ge(e_xT, e + 1)
                for k, dst in enumerate((Cp, Yp)):
                    if e:
                        pe.wait_ge((e_h0, e_h1)[k], e)
                    for c in (slice(0, HALF), slice(HALF, CAP)):
                        ins = te_.matmul(dst[:, c], w1s[:, e, k * P:(k + 1) * P], xT[:, e % 2, c], start=True,
                                         stop=True)
                    ins.then_inc(e_up, 1)

            def down(e):
                pe.wait_ge(e_h0, e + 1)
                pe.wait_ge(e_h1, e + 1)
                if e >= 2:
                    pe.wait_ge(e_y, e - 1)
                for k in range(ET):
                    for i, hid in enumerate((h0, h1)):
                        ins = te_.matmul((M0, M1)[e % 2][:, k * C:(k + 1) * C], hid[:, e % 2, k * P:(k + 1) * P],
                                         w2s[:, e, i, :], start=(i == 0), stop=(i == 1))
                ins.then_inc(e_dn, 1)

            pe.wait_ge(b_idx, B)
            for k in range(12):
                te_.matmul(Yp[:, HB[k % 2]], idn, delta[:, HB[k % 2]], start=True, stop=True)

            pe.wait_ge(e_zero, 1)
            turn(0)
            up(0)
            turn(1)
            down(0)
            up(1)
            for e in range(1, E):
                if e + 1 < E:
                    turn(e + 1)
                if e + 1 < E:
                    up(e + 1)
                down(e)

        @block.vector
        def _(dve):
            ve = nc.vector
            X = mybir.AxisListType.X
            def input_sum(k, c):
                dve.wait_ge((x_first, x_rest)[k], 16)
                ve.reduce_sum(fs[:, 0, c], xs_in[:, :, :, :].rearrange("p b t c -> p (b t) c")[:, c, :],
                              X).then_inc(n_sum, 1)

            def input_squares(k, c):
                dve.wait_ge(n_sq, k + 1)
                ve.reduce_sum(fs[:, 2, c], squares[:, c, :], X).then_inc(n_var, 1)

            def normed_tiles(f):
                dve.wait_ge(n_z, 1 if first(f) else 2)
                ve.tensor_copy(zt[:, :, 0:C], at_tiles(fz, f)).then_inc(f_z, 1)

            def front(f, n):
                if n == 9:
                    dve.wait_ge(f_hi, f + 1)
                    ve.tensor_tensor(rest[:, :, :], rows_psum(f), bc[:, :, 0, :], ALU.subtract).then_inc(f_rest, 1)
                    dve.wait_ge(f_rest, f + 1)
                    ve.tensor_copy(bc[:, :, 1, :], rest[:, :, :]).then_inc(f_mid, 1)
                    dve.wait_ge(f_mid, f + 1)
                    ve.tensor_tensor(bc[:, :, 2, :], rest[:, :, :], bc[:, :, 1, :], ALU.subtract).then_inc(f_lo, 1)
                if n == 14:
                    if first(f):
                        dve.wait_ge(f_ln, 1)
                        ve.tensor_tensor(tabs[:, :], bx[:, 1, :], tabs[:, :], ALU.subtract).then_inc(f_less, 1)
                    dve.wait_ge(f_less, f + 1)
                    dve.wait_ge(f_sq, f + 1)
                    ve.tensor_scalar(small[:, :], at(du, f), 2.0 ** -10, None, ALU.is_lt)
                    dve.drain()
                    ve.copy_predicated(tabs[:, :], small[:, :], te[:, :]).then_inc(f_pick, 1)
                if n == 15:
                    dve.wait_ge(f_pick, f + 1)
                    dve.wait_ge(f_high, f + 1)
                    if not first(f):
                        dve.wait_ge(s_dA, 16 * f)
                    ve.tensor_tensor(delta[:, :], trel[:, :], tabs[:, :], ALU.subtract).then_inc(f_delta, 1)
                    dve.wait_ge(f_delta, f + 1)
                    ve.tensor_tensor(at(du, f), delta[:, :], at(u, f), ALU.mult).then_inc(f_du, 1)

            def drive(s, n):
                dve.wait_ge(s_B, 16 * s + n + 1)
                ve.tensor_tensor(bx[:, n % 2, :], Bp[:, :], at(du, s), ALU.mult).then_inc(s_mul, 1)

            def scan(s, n):
                j, own = n // 2, n % 2 == 0
                hb = h[:, 0 if own else 1 + j % 2, :]
                if not own and not (first(s) and j < 2):
                    dve.wait_ge(s_pP, 8 * s + j - 1)
                dve.wait_ge(s_mul, 16 * s + n + 1)
                dve.wait_ge(s_dA, 16 * s + n + 1)
                ve.tensor_tensor_scan(hb, dA[:, n % 3, :], bx[:, n % 2, :], 0.0, ALU.mult, ALU.add).then_inc(s_scan, 1)
                if n + 1 < 16:
                    drive(s, n + 1)
                if own:
                    dve.wait_ge(s_scan, 16 * s + n + 1)
                    dve.wait_ge(s_C, 16 * s + n + 1)
                    if not (first(s) and j < 2):
                        dve.wait_ge(s_sum, 16 * s + n - 3)
                    ve.tensor_tensor(prod[:, j % 2, :], Cp[:, :], hb, ALU.mult).then_inc(s_pD, 1)

            def last_norm(k, src, dst, done):
                link, o = Chain(dve, l_dve, k, 4), 10 * k
                link(ve.tensor_scalar(bs[:, o + 1, :], bs[:, o, :], 1.0 / C, None, ALU.mult))
                link(ve.tensor_tensor(bxm[:, :, :], src, over(bs[:, o + 1, :], C), ALU.subtract))
                link(ve.tensor_tensor(dst, bxm[:, :, :], bxm[:, :, :], ALU.mult))
                link(ve.reduce_sum(bs[:, o + 2, :], dst, X))
                link.end()
                ve.tensor_scalar(bs[:, o + 4, :], bs[:, o + 2, :], 1.0 / C, LN_EPS, ALU.mult, ALU.add).then_inc(l_var, 1)
                dve.wait_ge(l_rstd, k + 1)
                ve.tensor_tensor(dst, bxm[:, :, :], over(bs[:, o + 5, :], C), ALU.mult).then_inc(done, 1)

            def back(g, n):
                if n == 0:
                    dve.wait_ge(s_sum, 16 * g + 16)
                    ve.scalar_tensor_tensor(yt[:, :], at(u, g), Dcol[:, :], Yp[:, :], ALU.mult,
                                            ALU.add).then_inc(b_yt, 1)
                    dve.wait_ge(b_yt, g + 1)
                    dve.wait_ge(f_gate, g + 1)
                    ve.tensor_tensor(yt[:, :], yt[:, :], at(sz, g), ALU.mult).then_inc(b_yg, 1)
                if n == 2:
                    dve.wait_ge(b_op, g + 1)
                    dve.wait_ge(f_skx, g + 1)
                    ve.tensor_tensor(y2[:, :, :], tiles(M0[:, :], C), at_tiles(skx, g), ALU.add).then_inc(b_y2, 1)
                    dve.wait_ge(b_y2, g + 1)
                    ve.reduce_sum(bs[:, 0, :], y2[:, :, :], X).then_inc(b_sum, 1)
                    if last(g):
                        dve.wait_ge(b_sum, g + 1)
                        last_norm(0, y2[:, :, :], n2[:, :, 0:C], b_n2)
                if not last(g) and n in (3, 8):
                    k = n // 8
                    dve.wait_ge((b_sq, b_sq3)[k], g + 1)
                    ve.reduce_sum(bs[:, 10 * k + 2, :], (n2, rows)[k][:, :, 0:C], X).then_inc((b_var, b_var3)[k], 1)
                if n == 7:
                    dve.wait_ge(b_pr, g + 1)
                    dve.wait_ge(b_sent, 16 + SENT * g)
                    if not first(g):
                        dve.wait_ge(b_res, 16 * g)
                    t1 = rows[:, :, R_RES:R_RES + C]
                    ve.tensor_tensor(t1, tiles(back_bank(g, "proj"), C), at_tiles(xs_in, g), ALU.add).then_inc(b_t1, 1)
                    dve.wait_ge(b_t1, g + 1)
                    ve.reduce_sum(bs[:, 10, :], t1, X).then_inc(b_sum3, 1)
                    if last(g):
                        dve.wait_ge(b_sum3, g + 1)
                        last_norm(1, t1, rows[:, :, 0:C], b_h3)
                if n == 13:
                    link = Chain(dve, b_dve, g, 3)
                    lg = tiles(back_bank(g, "gate")[:, 0:T * E], E)
                    dve.wait_ge(b_gate, g + 1)
                    link(ve.tensor_reduce(bs[:, 20, :], lg, X, ALU.max))
                    ve.tensor_tensor(ld[:, :, :], lg, over(bs[:, 20, :], E), ALU.subtract).then_inc(b_ld, 1)
                    dve.wait_ge(b_ld, g + 1)
                    link(ve.scalar_tensor_tensor(lrev[:, :, :], ld[:, :, :], 0.0, revc[:, :, :], ALU.is_equal,
                                                 ALU.mult))
                    link(ve.tensor_reduce(bs[:, 21, :], lrev[:, :, :], X, ALU.max))
                    link.end()
                    link = Chain(dve, b_dve2, g, 2)
                    link(ve.tensor_tensor(oh[:, :, 1:T + 1].rearrange("p e t -> p t e"), lrev[:, :, :],
                                          over(bs[:, 21, :], E), ALU.is_equal))
                    ve.tensor_tensor_scan(before[:, :, :].rearrange("p e t -> p (e t)"),
                                          resets[:, :, :].rearrange("p e t -> p (e t)"),
                                          oh[:, :, :].rearrange("p e t -> p (e t)"), 0.0, ALU.mult,
                                          ALU.add).then_inc(b_oh, 1)
                    dve.wait_ge(b_oh, g + 1)
                    link(ve.tensor_copy(oh[:, :, 0:1], before[:, :, T:T + 1]))
                    link.end()
                if n == 15:
                    dve.wait_ge(b_ex, g + 1)
                    link = Chain(dve, b_dve3, g, 7)
                    link(ve.reduce_sum(bs[:, 22, :], lex[:, :, :], X))
                    link(ve.reciprocal(rows[:, :, R_PRB:R_PRB + 1], bs[:, 22, :].unsqueeze(2)))
                    ve.tensor_copy(rows[:, :, R_ID:R_ID + 1].bitcast(I32), ids[:, bass.ds(g, 1), :].rearrange(
                        "p b t -> p t b"))
                    link(ve.tensor_scalar(bs[:, 23, :], bs[:, 21, :], -float(CAP), float(E * CAP), ALU.mult, ALU.add))
                    dve.wait_ge(b_pos, g + 1)
                    link(ve.tensor_tensor(lpo[:, :, :], M1[:, T * E:2 * T * E].rearrange("p (e t) -> p t e", e=E),
                                          oh[:, :, 1:T + 1].rearrange("p e t -> p t e"), ALU.mult))
                    link(ve.reduce_sum(bs[:, 24, :], lpo[:, :, :], X))
                    link(ve.tensor_scalar(bs[:, 25, :], bs[:, 24, :], float(CAP), float(2 * E * CAP), ALU.is_ge,
                                          ALU.mult))
                    link(ve.tensor_tensor(bs[:, 26, :], bs[:, 24, :], bs[:, 23, :], ALU.add))
                    link.end()
                    ve.tensor_tensor(chosen[:, :], bs[:, 26, :], bs[:, 25, :], ALU.add).then_inc(b_idx, 1)

            one, rest_of_x = slice(0, T), slice(T, B * T)
            ve.memset(w1s[C:P, :, :], 0.0)
            input_sum(0, one)
            dve.wait_ge(w_first, 16 * 5)
            for k in range(TAPS):
                ins = ve.tensor_scalar(taps[:, k, :], wi[:, 0, :], cw[:, k:k + 1], None, ALU.mult)
            ins.then_inc(taps_done, 1)
            input_squares(0, one)
            dve.wait_ge(conv_tr, 1)
            for dst, src in ((tapA[:, :], Cp[:, 0:128]), (tapB[:, :], Cp[:, 128:256]), (wzT[:, :], Cp[0:C, 256:384])):
                ins = ve.tensor_copy(dst, src)
            ins.then_inc(conv_ev, 1)
            normed_tiles(0)
            dve.wait_ge(w_in, 16 * 13)
            dve.wait_ge(pool_const, 4)
            ve.tensor_scalar(gfold[:, 0:C], ident[0:C, 0:C], gcol[:, :], None, ALU.mult)
            ve.tensor_copy(gfold[:, C:C + 1], bcol[:, :])
            ve.tensor_copy(identb[:, :], ident[:, :])
            ve.tensor_scalar(gskip[:, :], gskip[:, :], skcol[:, :], None, ALU.mult)
            ve.tensor_scalar(bskip[:, :], bskip[:, :], skcol[:, :], None, ALU.mult).then_inc(w_fold, 1)
            input_sum(1, rest_of_x)
            dve.wait_ge(w_tr, 1)
            for dst, src in ((bcT[:, :], Bp[:, 384:416]), (dtwT[:, :], Bp[0:R, 512:640]), (woT[:, :], Bp[:, 640:704]),
                             (pwT[:, :], Bp[0:C, 704:768]), (b1c[:, :], Bp[:, 768:784])):
                ins = ve.tensor_copy(dst, src)
            ins.then_inc(w_ev, 1)
            dve.wait_ge(w_mm, 1)
            ve.tensor_copy(wdt[:, :], Bp[:, 0:P])
            ve.tensor_copy(PW[:, :], Bp[0:C + 1, 784:784 + C]).then_inc(w_ready, 1)
            ve.tensor_copy(sel[:, :, :], sel1[:, :].unsqueeze(2).broadcast_to([96, 2 * N, P])).then_inc(sel_done, 1)
            dve.wait_ge(a_exp, 1)
            ve.tensor_scalar(aneg[:, :], aneg[:, :], -1.0, None, ALU.mult).then_inc(aneg_done, 1)
            for q in range(2):
                dve.wait_ge(f_abs, q + 1)
                ve.tensor_scalar(trel[:, HB[q]], bank(0, "step", q), dtb[:, :], 0.0, ALU.add, ALU.max)
            input_squares(1, rest_of_x)
            dve.wait_ge(f_exp, 1)
            ve.tensor_scalar(bx[:, 0, :], at(du, 0), 1.0, None, ALU.add).then_inc(f_one, 1)
            dve.wait_ge(f_one, 1)
            ve.tensor_scalar(bx[:, 1, :], bx[:, 0, :], -1.0, None, ALU.add)
            ve.tensor_tensor(trel[:, :], trel[:, :], at(du, 0), ALU.add).then_inc(f_high, 1)
            dve.wait_ge(f_high, 1)
            for n in (9, 14, 15):
                front(0, n)

            def step(s, has_front, has_back):
                dve.wait_ge(f_du, s + 1)
                drive(s, 0)
                if has_front:
                    normed_tiles(s + 1)
                for n in range(16):
                    scan(s, n)
                    if has_back:
                        back(s - 1, n)
                    if has_front:
                        front(s + 1, n)
                if has_back:
                    back(s - 1, 16)

            step(0, True, False)
            with dve.Fori(1, B - 1) as s:
                step(s, True, True)
            step(B - 1, False, True)
            for n in range(17):
                back(B - 1, n)

            ve.memset(xT[C:P, :, :], 0.0).then_inc(e_zero, 1)
            dve.wait_ge(late_in, 16 * 5)
            for e in range(E):
                link = Chain(dve, e_dve, e, 4)
                y, cl, ok, diff = (ye[:, i] for i in range(4))
                dve.wait_ge(e_dn, e + 1)
                ve.tensor_tensor(y, tiles((M0, M1)[e % 2][:, 0:ET * C], C, ET),
                                 b2s[:, e, :].unsqueeze(1).broadcast_to([P, ET, C]), ALU.add).then_inc(e_y, 1)
                dve.wait_ge(e_y, e + 1)
                link(ve.tensor_tensor(y, y, xe[e][:, :, R_PRB:R_PRB + 1].broadcast_to([P, ET, C]), ALU.mult))
                ve.tensor_tensor(diff, y, y, ALU.subtract).then_inc(e_diff, 1)
                ve.tensor_scalar(cl, y, 1e4, -1e4, ALU.min, ALU.max)
                link(ve.tensor_tensor(ok, y, y, ALU.is_equal))
                dve.wait_ge(e_diff, e + 1)
                ve.tensor_scalar(fin[:, :, :], diff, 0.0, None, ALU.is_equal)
                link(ve.tensor_tensor(cl, cl, ok, ALU.mult))
                link(ve.copy_predicated(cl, fin[:, :, :], y))
                if e >= 2:
                    dve.wait_ge(e_out[e % 2], 16 * ET * (e // 2))
                ve.tensor_tensor(yo[:, e % 2], cl, xe[e][:, :, R_RES:R_RES + C], ALU.add).then_inc(e_yo, 1)
                link.end()


_INS = ['x', 'L0_conv_ln_g', 'L0_conv_ln_b', 'L0_conv_in_proj_w', 'L0_conv_conv_w', 'L0_conv_conv_b',
        'L0_conv_x_proj_w', 'L0_conv_dt_proj_w', 'L0_conv_dt_proj_b', 'L0_conv_A_log', 'L0_conv_D',
        'L0_conv_out_proj_w', 'L0_conv_proj_w', 'L0_conv_proj_b', 'L0_conv_skip_scale', 'L0_ffn_gate_w',
        'L0_ffn_gate_b', 'L0_ffn_w1', 'L0_ffn_b1', 'L0_ffn_w2', 'L0_ffn_b2']
_OUTS = [((4, 32, 32, 64), 'float32')]


def kernel(**inputs):
    import numpy as _np
    import concourse.bacc as _bacc
    from concourse import mybir as _mybir
    from concourse.bass_utils import run_bass_kernel_spmd as _run

    nc = _bacc.Bacc("TRN2", target_bir_lowering=False, num_devices=1)
    arrays, args = {}, []
    for name in _INS:
        a = _np.ascontiguousarray(inputs[name])
        arrays[f"in_{name}_dram"] = a
        args.append(nc.dram_tensor(f"in_{name}_dram", a.shape, _mybir.dt.from_np(a.dtype), kind="ExternalInput").ap())
    for i, (shape, dtype) in enumerate(_OUTS):
        dt = _mybir.dt.from_np(_np.dtype(dtype))
        args.append(nc.dram_tensor(f"out_{i}_dram", shape, dt, kind="ExternalOutput").ap())
    metaformer_layer(nc, *args)
    r = _run(nc, [arrays], core_ids=[0])
    got = tuple(r.results[0][f"out_{i}_dram"] for i in range(len(_OUTS)))
    return got[0]
```
